# Optimizing a Trainium2 kernel written in Bass

```python
import numpy as np
import jax
import jax.numpy as jnp

def _softmax(x, axis=-1):
    return jax.nn.softmax(x, axis=axis)

def _gelu(x):
    return jax.nn.gelu(x, approximate=True)

def _silu(x):
    return jax.nn.silu(x)

def _sigmoid(x):
    return jax.nn.sigmoid(x)

def _layernorm(x, axis=-1, eps=1e-05):
    m = jnp.mean(x, axis=axis, keepdims=True)
    v = jnp.var(x, axis=axis, keepdims=True)
    return (x - m) / jnp.sqrt(v + eps)

def _scatter_add(tgt, idx, src, axis=0):
    return tgt.at[idx].add(src)

def _segment_sum(src, seg, n):
    return jax.ops.segment_sum(src, seg, n)
kernel_name = 'mk_adj_preln_d1_adj_r2_ff9b28'

def setup_inputs(seed: int=0):
    np.random.seed(seed)
    _w = jnp.asarray

    def _rec_inputs():
        import jax
        import jax.numpy as jnp
        _gk = jax.random.key(seed)
        x = -0.0005963 + 1.001 * jax.random.normal(jax.random.fold_in(_gk, 1), (2048, 256), jnp.float32)
        _w = (1.0 + jnp.arange(2048, dtype=jnp.float32)) ** (-0.5)
        _w = _w / _w.mean()
        _pij = jnp.clip(0.0078125 * _w[:, None] * _w[None, :], 0.0, 1.0)
        _a = jax.random.uniform(jax.random.fold_in(_gk, 2), (2048, 2048)) < _pij
        _af = _a.astype(jnp.float32)
        adj = _af
        return (x, adj)
    x, adj = _rec_inputs()

    def _L0_gnn_setup():
        import jax, jax.numpy as jnp
        import numpy as np
        N = 3072
        D_IN = 256
        D_OUT = 256
        DENSITY = 0.005
        key = jax.random.key(seed)
        ks = jax.random.split(key, 12)
        x = jax.random.normal(ks[0], (N, D_IN), dtype=jnp.float32)
        adj_a = (jax.random.uniform(ks[1], (N, N)) < DENSITY).astype(jnp.float32)
        adj_b = (jax.random.uniform(ks[2], (N, N)) < DENSITY).astype(jnp.float32)
        W_sa = jax.random.normal(ks[3], (D_IN, D_OUT), dtype=jnp.float32) * (1.414 / np.sqrt(D_IN + D_OUT))
        a_sa = jax.random.normal(ks[4], (1, 2 * D_OUT), dtype=jnp.float32) * (1.414 / np.sqrt(1 + 2 * D_OUT))
        stdv = 1.0 / np.sqrt(D_OUT)
        W_gcnb = jax.random.uniform(ks[5], (D_IN, D_OUT), minval=-stdv, maxval=stdv, dtype=jnp.float32)
        b_gcnb = jax.random.uniform(ks[6], (D_OUT,), minval=-stdv, maxval=stdv, dtype=jnp.float32)
        s = 1.0 / np.sqrt(2 * D_IN)
        Wa = jax.random.uniform(ks[7], (1, 2 * D_IN), minval=-s, maxval=s, dtype=jnp.float32)
        ba = jax.random.uniform(ks[8], (1,), minval=-s, maxval=s, dtype=jnp.float32)
        Wb = jax.random.uniform(ks[9], (1, 2 * D_IN), minval=-s, maxval=s, dtype=jnp.float32)
        bb = jax.random.uniform(ks[10], (1,), minval=-s, maxval=s, dtype=jnp.float32)
        return {'x': x, 'adj_a': adj_a, 'adj_b': adj_b, 'W_sa': W_sa, 'a_sa': a_sa, 'W_gcnb': W_gcnb, 'b_gcnb': b_gcnb, 'Wa': Wa, 'ba': ba, 'Wb': Wb, 'bb': bb}
    _L0_gnn_all = _L0_gnn_setup()
    _L0_gnn_in = {k: v for k, v in _L0_gnn_all.items() if k in ('W_sa', 'a_sa', 'W_gcnb', 'b_gcnb', 'Wa', 'ba', 'Wb', 'bb')}
    del _L0_gnn_all
    return {'x': x, 'adj': adj, 'L0_gnn_W_sa': _L0_gnn_in['W_sa'], 'L0_gnn_a_sa': _L0_gnn_in['a_sa'], 'L0_gnn_W_gcnb': _L0_gnn_in['W_gcnb'], 'L0_gnn_b_gcnb': _L0_gnn_in['b_gcnb'], 'L0_gnn_Wa': _L0_gnn_in['Wa'], 'L0_gnn_ba': _L0_gnn_in['ba'], 'L0_gnn_Wb': _L0_gnn_in['Wb'], 'L0_gnn_bb': _L0_gnn_in['bb']}

def reference(x, adj, L0_gnn_W_sa, L0_gnn_a_sa, L0_gnn_W_gcnb, L0_gnn_b_gcnb, L0_gnn_Wa, L0_gnn_ba, L0_gnn_Wb, L0_gnn_bb):
    import jax
    import jax.numpy as jnp

    def _L0_gnn_ref(x, adj_a, adj_b, W_sa, a_sa, W_gcnb, b_gcnb, Wa, ba, Wb, bb):
        import jax, jax.numpy as jnp
        import numpy as np
        N = 3072
        D_IN = 256
        D_OUT = 256
        DENSITY = 0.005
        type_sum_a = adj_a @ x
        type_sum_b = adj_b @ x
        attn_a = jax.nn.sigmoid(jnp.concatenate([type_sum_a, x], axis=1) @ Wa.T + ba)
        attn_b = jax.nn.sigmoid(jnp.concatenate([type_sum_b, x], axis=1) @ Wb.T + bb)
        h = x @ W_sa
        Hd = h.shape[1]
        s_left = h @ a_sa[0, :Hd]
        s_right = h @ a_sa[0, Hd:]
        scores = s_left[:, None] + s_right[None, :]
        e = jnp.where(adj_a != 0, jnp.exp(-jax.nn.leaky_relu(scores, 0.01)), 0.0)
        attn = e / (jnp.sum(e, axis=1, keepdims=True) + 1e-05)
        x_a = attn @ h
        x_b = adj_b @ (x @ W_gcnb) + b_gcnb
        return jax.nn.sigmoid(attn_a * x_a + attn_b * x_b)
    h = jnp.maximum(_layernorm(x, axis=-1), 0.0)
    x = x + _L0_gnn_ref(h, adj, adj, L0_gnn_W_sa, L0_gnn_a_sa, L0_gnn_W_gcnb, L0_gnn_b_gcnb, L0_gnn_Wa, L0_gnn_ba, L0_gnn_Wb, L0_gnn_bb)
    return x

_drawn_inputs = setup_inputs


def setup_inputs(seed=0):
    import zlib

    import numpy as np

    out = dict(_drawn_inputs(seed))
    spreads = {}
    factors = {'L0_gnn_W_sa': 2.942, 'L0_gnn_a_sa': 8.0, 'L0_gnn_b_gcnb': 23.426, 'L0_gnn_Wa': 4.262}
    for name, (base, spread) in spreads.items():
        noise = np.random.default_rng([zlib.crc32(name.encode()), seed]).standard_normal(out[name].shape)
        drawn = base * np.exp(spread * noise) if base else spread * noise
        out[name] = jnp.asarray(drawn.astype(out[name].dtype))
    for name, factor in factors.items():
        out[name] = (out[name] * factor).astype(out[name].dtype)
    return out
```

```python
from contextlib import ExitStack
import math

import concourse.bass as bass
from concourse import mybir

F32 = mybir.dt.float32
F16 = mybir.dt.float16
I32 = mybir.dt.int32
ALU = mybir.AluOpType
ACT = mybir.ActivationFunctionType

P = 128
N = 2048
D = 256
NT = N // P
KT = D // P
GT = 4
NG = NT // GT
CW = 256
NCH = N // CW
TPC = CW // P
NP = NT // 2
RING = 4
BANK = 512

LO = 2.0 ** 11
H0_SCALE = 2.0 ** 6
W_SCALE = LO / H0_SCALE
E_SCALE = 2.0 ** 6
LOG_E = math.log(E_SCALE * LO)
LN_EPS = 1e-5
RSQRT_STEPS = 12
SUM_EPS = 1e-5
SLOPE = 0.01

SL, SR, UA, UB, CA, CB = range(6)
NX = 6
C_AVEC, C_GATE, C_BAB, C_BIAS = 0, 4, 12, 14
C_END = C_BIAS + D


def build(nc, x, adj_t, weights, consts, out):
    with ExitStack() as ctx:
        def sb(name, shape, dt):
            return ctx.enter_context(nc.sbuf_tensor(name, shape, dt))

        def sem(name):
            return ctx.enter_context(nc.semaphore(name))

        ps = ctx.enter_context(nc.psum_tensor("ps", [P, 8, BANK], F32))

        w_sb = sb("w_sb", [P, KT, 3, D], F32)
        c_sb = sb("c_sb", [P, C_END], F32)
        w_hi = sb("w_hi", [P, KT, 2, D], F16)
        w_lo = sb("w_lo", [P, KT, 2, D], F16)
        wx = sb("wx", [P, KT, NX], F32)
        wx_hi = sb("wx_hi", [P, KT, NX], F16)
        wx_lo = sb("wx_lo", [P, KT, NX], F16)
        wrep_hi = sb("wrep_hi", [P, KT, P], F16)
        wrep_lo = sb("wrep_lo", [P, KT, P], F16)
        ident = sb("ident", [P, P], F32)
        x_sb = sb("x_sb", [P, NT, D], F32)
        stats = sb("stats", [P, NT, 6], F32)
        mean_var = sb("mean_var", [P, NT, 2], F32)
        rstd = sb("rstd", [P, NG, GT], F32)
        rs_v = sb("rs_v", [P, NG, GT], F32)
        rs_a = sb("rs_a", [P, NG, GT], F32)
        xn = sb("xn", [P, 2, GT, D], F32)
        h0t_hi = sb("h0t_hi", [P, KT, N], F16)
        h0t_lo = sb("h0t_lo", [P, KT, N], F16)
        mv_hi = sb("mv_hi", [P, NT, 2, D + 2], F16)
        mv_lo = sb("mv_lo", [P, NT, 2, D + 2], F16)
        exs = sb("exs", [P, NT, NX], F32)
        sr_col = sb("sr_col", [P, NT], F32)
        factor_arg = sb("factor_arg", [P, NT, 2], F32)
        factor = sb("factor", [P, NT, 2], F32)
        log_e = sb("log_e", [P, 1], F32)
        gate_c = sb("gate_c", [P, NT, 2], F32)
        sl_row = sb("sl_row", [P, N + CW], F32)
        sl_now = sb("sl_now", [P, 2, CW], F32)
        adj16 = sb("adj16", [P, 2, NT, CW], F16)
        e_raw = sb("e_raw", [P, RING, 2, CW], F32)
        e_msk = sb("e_msk", [P, RING, 2, CW], F32)
        e_hi = sb("e_hi", [P, 2, NT, CW], F16)
        e_lo = sb("e_lo", [P, 2, NT, CW], F16)
        low_a = sb("low_a", [P, 2, D + 2], F32)
        low_b = sb("low_b", [P, 2, D + 2], F32)
        sum_a = sb("sum_a", [P, 2, D + 2], F32)
        sum_b = sb("sum_b", [P, 2, D + 2], F32)
        small = sb("small", [P, 2, 8], F32)
        part_a = sb("part_a", [P, 2, D], F32)
        part_b = sb("part_b", [P, 2, D], F32)
        logit = sb("logit", [P, 2, D], F32)
        tanh_v = sb("tanh_v", [P, 2, D], F32)
        res = sb("res", [P, 2, D], F32)

        w_landed = sem("w_landed")
        c_landed = sem("c_landed")
        x_landed = [sem(f"x_landed{g}") for g in range(NG)]
        adj_landed = [[sem(f"adj_landed{s}{h}") for h in range(2)] for s in range(2)]
        ident_ready = sem("ident_ready")
        wl_product = sem("wl_product")
        wx_scaled = sem("wx_scaled")
        wx_high = sem("wx_high")
        wx_ready = sem("wx_ready")
        w_high = sem("w_high")
        w_ready = sem("w_ready")
        ones_ready = sem("ones_ready")
        stats_done = sem("stats_done")
        moments_done = sem("moments_done")
        rstd_done = sem("rstd_done")
        normed = sem("normed")
        xh_ready = sem("xh_ready")
        turned = sem("turned")
        h0t_high = sem("h0t_high")
        h0t_ready = sem("h0t_ready")
        sl_product = sem("sl_product")
        sl_ready = sem("sl_ready")
        sl_now_ready = sem("sl_now_ready")
        narrow_product = sem("narrow_product")
        narrow_copied = sem("narrow_copied")
        narrow_high = sem("narrow_high")
        narrow_ready = sem("narrow_ready")
        factor_args = sem("factor_args")
        factors_done = sem("factors_done")
        eps_ready = sem("eps_ready")
        wide_product = sem("wide_product")
        wide_high = sem("wide_high")
        wide_ready = sem("wide_ready")
        relu_done = sem("relu_done")
        exp_done = sem("exp_done")
        masked = sem("masked")
        e_high = sem("e_high")
        e_ready = sem("e_ready")
        banks_free = sem("banks_free")
        tile_done = sem("tile_done")
        low_copied = sem("low_copied")
        summed = sem("summed")
        gate_arg = sem("gate_arg")
        den_done = sem("den_done")
        rden_done = sem("rden_done")
        gate_tanh = sem("gate_tanh")
        gates_done = sem("gates_done")
        scaled = sem("scaled")
        logits_done = sem("logits_done")
        tanh_done = sem("tanh_done")
        res_ready = sem("res_ready")
        stored = [sem(f"stored{q}") for q in range(TPC)]

        adj_v = adj_t.rearrange("(j p) i -> p j i", p=P)
        x_v = x.rearrange("(t p) d -> p t d", p=P)

        def t_bank(g, k):
            return ps[:, 2 * (g % 2) + k, :]

        def wide_bank(t):
            return ps[:, 4 + t % 2, :].rearrange("p (m d) -> p m d", m=2)

        sl_bank = ps[:, 6, :]
        narrow_bank = ps[:, 7, 0:8 * GT].rearrange("p (t n) -> p t n", n=8)
        wl_bank = ps[:, 7, 0:2 * KT].rearrange("p (k n) -> p k n", k=KT)

        def out_bank(q, b):
            return ps[:, 4 * q + b, :]

        block = ctx.enter_context(nc.Block())

        @block.sync
        def _(sp):
            sp.dma_start(c_sb[:, :], consts).then_inc(c_landed, 16)
            for g in range(NG):
                sp.dma_start(x_sb[:, g * GT:(g + 1) * GT, :], x_v[:, g * GT:(g + 1) * GT, :]).then_inc(x_landed[g], 16)
            with sp.Fori(0, NCH) as c:
                for q in range(TPC):
                    sp.wait_ge(res_ready, c * TPC + q + 1)
                    sp.dma_start(out[bass.ds((c * TPC + q) * P, P), :], res[:, q, :]).then_inc(stored[q], 16)
            for q in range(TPC):
                sp.wait_ge(stored[q], 16 * NCH)

        @block.gpsimd
        def _(pool):
            def load_adj(slot, c):
                for half in range(2):
                    js = slice(half * NT // 2, (half + 1) * NT // 2)
                    pool.dma_start(adj16[:, slot, js, :], adj_v[:, js, bass.ds(c * CW, CW)])\
                        .then_inc(adj_landed[slot][half], 16)

            pool.memset(ident[:, :], 0.0).then_inc(ident_ready, 1)
            load_adj(0, 0)
            pool.wait_ge(ident_ready, 1)
            pool.affine_select(out=ident[:, :], in_=ident[:, :], compare_op=ALU.not_equal, fill=1.0,
                               base=0, pattern=[[-1, P]], channel_multiplier=1).then_inc(ident_ready, 1)
            load_adj(1, 1)
            for g in range(NG):
                pool.wait_ge(normed, (g + 1) * GT)
                xs = x_sb[:, g * GT:(g + 1) * GT, :]
                pool.tensor_scalar(xs, xs, 0.5, None, ALU.add).then_inc(xh_ready, 1)
            with pool.Fori(0, NCH // 2 - 1) as r:
                for slot in range(2):
                    pool.wait_ge(tile_done, r * 2 * TPC + (slot + 1) * TPC)
                    load_adj(slot, r * 2 + slot + 2)

        def relu_pair(act, c_slot, p, n):
            if n is not None:
                act.wait_ge(masked, n - RING + 1)
            for u in range(2):
                j = 2 * p + u
                ins = act.activation(e_raw[:, p % RING, u, :], sl_now[:, c_slot, :], ACT.Relu,
                                     bias=sr_col[:, j:j + 1], scale=1.0 / LO)
            ins.then_inc(relu_done, 1)

        def exp_pair(act, p, n):
            act.wait_ge(relu_done, n + 1)
            act.activation(e_raw[:, p % RING, :, :], e_raw[:, p % RING, :, :], ACT.Exp,
                           bias=log_e[:, 0:1], scale=SLOPE - 1.0)\
                .then_inc(exp_done, 1)

        def next_sl(act, c_slot, c):
            act.activation(sl_now[:, c_slot, :], sl_row[:, bass.ds(c * CW, CW)], ACT.Copy).then_inc(sl_now_ready, 1)

        def high_pair(act, c_slot, p, n):
            act.wait_ge(masked, n + 1)
            act.activation(e_hi[:, c_slot, 2 * p:2 * p + 2, :], e_msk[:, p % RING, :, :], ACT.Copy,
                           scale=1.0 / LO).then_inc(e_high, 1)

        def mask_pair(dve, c_slot, p, n, wait_ring):
            dve.wait_ge(exp_done, n + 1)
            if wait_ring:
                dve.wait_ge(e_high, n - RING + 1)
            for u in range(2):
                j = 2 * p + u
                ins = dve.scalar_tensor_tensor(out=e_msk[:, p % RING, u, :], in0=e_raw[:, p % RING, u, :],
                                               scalar=factor[:, j, 0:1], in1=adj16[:, c_slot, j, :],
                                               op0=ALU.mult, op1=ALU.mult)
            ins.then_inc(masked, 1)

        def low_pair(dve, c_slot, p, n):
            dve.wait_ge(e_high, n + 1)
            dve.scalar_tensor_tensor(out=e_lo[:, c_slot, 2 * p:2 * p + 2, :], in0=e_hi[:, c_slot, 2 * p:2 * p + 2, :],
                                     scalar=-LO, in1=e_msk[:, p % RING, :, :],
                                     op0=ALU.mult, op1=ALU.add).then_inc(e_ready, 1)

        def act_low(act, q, n):
            act.wait_ge(tile_done, n + 1)
            act.activation(low_a[:, q, 0:D + 1], out_bank(q, 1)[:, 0:D + 1], ACT.Copy, scale=1.0 / LO)
            act.activation(low_b[:, q, :], out_bank(q, 3)[:, 0:D + 2], ACT.Copy, scale=1.0 / LO).then_inc(low_copied, 1)

        def act_gates(act, q, n):
            act.wait_ge(gate_arg, n + 1)
            act.activation(small[:, q, 2:4], small[:, q, 0:2], ACT.Tanh, scale=0.5).then_inc(gate_tanh, 1)

        def act_tanh(act, q, n):
            act.wait_ge(logits_done, n + 1)
            act.activation(tanh_v[:, q, :], logit[:, q, :], ACT.Tanh, scale=0.5).then_inc(tanh_done, 1)

        def dve_sum(dve, q, n, t):
            dve.wait_ge(low_copied, n + 1)
            dve.tensor_tensor(sum_b[:, q, :], low_b[:, q, :], out_bank(q, 2)[:, 0:D + 2], ALU.add)
            dve.tensor_tensor(sum_a[:, q, 0:D + 1], low_a[:, q, 0:D + 1], out_bank(q, 0)[:, 0:D + 1], ALU.add)\
                .then_inc(banks_free, 1)
            dve.wait_ge(banks_free, n + 1 + TPC)
            dve.tensor_tensor(small[:, q, 0:2], sum_b[:, q, D:D + 2], gate_c[:, t, :], ALU.add).then_inc(gate_arg, 1)
            dve.tensor_tensor(small[:, q, 4:5], sum_a[:, q, D:D + 1], factor[:, t, 1:2], ALU.add).then_inc(den_done, 1)
            dve.tensor_tensor(part_b[:, q, :], sum_b[:, q, 0:D], c_sb[:, C_BIAS:C_END], ALU.add)
            dve.wait_ge(den_done, n + 1)
            dve.reciprocal(small[:, q, 5:6], small[:, q, 4:5]).then_inc(rden_done, 1)

        def dve_logits(dve, q, n):
            dve.wait_ge(gate_tanh, n + 1)
            dve.tensor_scalar(small[:, q, 6:8], small[:, q, 2:4], 0.5, 0.5, ALU.mult, ALU.add).then_inc(gates_done, 1)
            dve.wait_ge(gates_done, n + 1)
            dve.wait_ge(rden_done, n + 1)
            dve.tensor_scalar(part_a[:, q, :], sum_a[:, q, 0:D], small[:, q, 5:6], small[:, q, 6:7],
                              ALU.mult, ALU.mult).then_inc(scaled, 1)
            dve.wait_ge(scaled, n + 1)
            dve.scalar_tensor_tensor(out=logit[:, q, :], in0=part_b[:, q, :], scalar=small[:, q, 7:8],
                                     in1=part_a[:, q, :], op0=ALU.mult, op1=ALU.add).then_inc(logits_done, 1)

        def dve_result(dve, q, n, t, stores):
            dve.wait_ge(tanh_done, n + 1)
            if stores is not None:
                dve.wait_ge(stored[q], stores)
            dve.scalar_tensor_tensor(out=res[:, q, :], in0=tanh_v[:, q, :], scalar=0.5, in1=x_sb[:, t, :],
                                     op0=ALU.mult, op1=ALU.add).then_inc(res_ready, 1)

        @block.scalar
        def _(act):
            act.dma_start(w_sb[:, :, :, :], weights).then_inc(w_landed, 16)
            act.wait_ge(w_landed, 16)
            for k in range(KT):
                act.activation(w_hi[:, k, :, :], w_sb[:, k, 1:3, :], ACT.Copy, scale=W_SCALE).then_inc(w_high, 1)
            for g in range(NG):
                tg = slice(g * GT, (g + 1) * GT)
                cols = slice(g * GT * P, (g + 1) * GT * P)
                act.wait_ge(turned, g + 1)
                for k in range(KT):
                    act.activation(h0t_hi[:, k, cols], t_bank(g, k), ACT.Relu).then_inc(h0t_high, 1)
                act.wait_ge(sl_product, g + 1)
                act.activation(sl_row[:, cols], sl_bank, ACT.Copy).then_inc(sl_ready, 1)
                act.wait_ge(factor_args, g + 1)
                act.activation(factor[:, tg, :], factor_arg[:, tg, :], ACT.Exp).then_inc(factors_done, 1)
                if g == 0:
                    act.wait_ge(ones_ready, 2)
                    act.wait_ge(sl_ready, 1)
                    next_sl(act, 0, 0)
                    act.wait_ge(sl_now_ready, 1)
                for p in range(2 * g, 2 * g + 2):
                    relu_pair(act, 0, p, p if p >= RING else None)
                for p in range(2 * g, 2 * g + 2):
                    exp_pair(act, p, p)
                for t in range(g * GT, (g + 1) * GT):
                    act.wait_ge(wide_product, t + 1)
                    act.activation(mv_hi[:, t, :, 0:D], wide_bank(t), ACT.Copy, scale=1.0 / LO).then_inc(wide_high, 1)
                for p in range(2 * g, 2 * g + 2):
                    high_pair(act, 0, p, p)

            def step(slot, c, tiles, more=True):
                act.wait_ge(sl_now_ready, c + 1)
                act.wait_ge(tile_done, (c - 1) * TPC)
                for p in range(NP):
                    relu_pair(act, slot, p, c * NP + p)
                    if p >= 1:
                        exp_pair(act, p - 1, c * NP + p - 1)
                    if p >= 2:
                        high_pair(act, slot, p - 2, c * NP + p - 2)
                    for at, q, n in tiles:
                        if p == at:
                            act_low(act, q, n)
                        if p == at + 1:
                            act_gates(act, q, n)
                        if p == at + 2:
                            act_tanh(act, q, n)
                exp_pair(act, NP - 1, c * NP + NP - 1)
                high_pair(act, slot, NP - 2, c * NP + NP - 2)
                high_pair(act, slot, NP - 1, c * NP + NP - 1)
                if more:
                    next_sl(act, 1 - slot, c + 1)

            act.wait_ge(sl_ready, NG)
            next_sl(act, 1, 1)
            step(1, 1, [(4, 0, 0)])
            with act.Fori(0, NCH // 2 - 1) as r:
                for s in range(2):
                    step(s, r * 2 + s + 2, [(0, 1, r * 2 * TPC + s * TPC + 1), (4, 0, r * 2 * TPC + s * TPC + 2)])
            for n in range(NT - 3, NT):
                act_low(act, n % 2, n)
                act_gates(act, n % 2, n)
                act_tanh(act, n % 2, n)

        @block.vector
        def _(dve):
            def rsqrt(g):
                v, y, a = (rs_v[:, g, :], rstd[:, g, :], rs_a[:, g, :])
                chain = [g * RSQRT_STEPS]

                def then(ins):
                    ins.then_inc(rstd_done, 1)
                    chain[0] += 1
                    dve.wait_ge(rstd_done, chain[0])

                then(dve.tensor_scalar(v, mean_var[:, g * GT:(g + 1) * GT, 1], LN_EPS, H0_SCALE ** -2, ALU.add, ALU.mult))
                then(dve.tensor_scalar(a.bitcast(I32), v.bitcast(I32), 1, None, ALU.logical_shift_right))
                then(dve.tensor_scalar(y.bitcast(I32), a.bitcast(I32), -1.0, float(0x5f3759df), ALU.mult, ALU.add))
                for _ in range(3):
                    then(dve.tensor_tensor(a, y, y, ALU.mult))
                    then(dve.scalar_tensor_tensor(out=a, in0=a, scalar=-0.5, in1=v, op0=ALU.mult, op1=ALU.mult))
                    then(dve.scalar_tensor_tensor(out=y, in0=a, scalar=1.5, in1=y, op0=ALU.add, op1=ALU.mult))

            def norm_group(g):
                tg = slice(g * GT, (g + 1) * GT)
                dve.wait_ge(x_landed[g], 16)
                for t in range(g * GT, (g + 1) * GT):
                    dve.bn_stats(stats[:, t, :], x_sb[:, t, :]).then_inc(stats_done, 1)
                for t in range(g * GT, (g + 1) * GT):
                    dve.wait_ge(stats_done, t + 1)
                    dve.bn_aggr(mean_var[:, t, :], stats[:, t, :]).then_inc(moments_done, 1)
                dve.wait_ge(moments_done, (g + 1) * GT)
                rsqrt(g)
                if g >= 2:
                    dve.wait_ge(turned, g - 1)
                for t in range(g * GT, (g + 1) * GT):
                    dve.tensor_scalar(xn[:, g % 2, t % GT, :], x_sb[:, t, :], mean_var[:, t, 0:1], rstd[:, g, t % GT:t % GT + 1],
                                      ALU.subtract, ALU.mult).then_inc(normed, 1)

            dve.memset(log_e[:, :], LOG_E)
            dve.memset(sl_row[:, N:N + CW], 0.0).then_inc(ones_ready, 1)
            dve.memset(mv_hi[:, :, 0, D:D + 1], 1.0)
            dve.memset(mv_lo[:, :, 0, D:D + 2], 0.0)
            dve.memset(mv_hi[:, :, 0, D + 1:D + 2], 0.0).then_inc(ones_ready, 1)
            dve.wait_ge(c_landed, 16)
            dve.tensor_scalar(wx[:, :, UA:UA + 4], c_sb[:, C_GATE:C_GATE + 4 * KT].rearrange("p (k n) -> p k n", k=KT),
                              W_SCALE, None, ALU.mult).then_inc(wx_scaled, 1)
            dve.wait_ge(wl_product, 1)
            dve.tensor_scalar(wx[:, :, 0:2], wl_bank, W_SCALE, None, ALU.mult).then_inc(wx_scaled, 1)
            dve.wait_ge(wx_scaled, 2)
            dve.tensor_copy(wx_hi[:, :, :], wx[:, :, :]).then_inc(wx_high, 1)
            dve.wait_ge(wx_high, 1)
            dve.tensor_tensor(wx_lo[:, :, :], wx[:, :, :], wx_hi[:, :, :], ALU.subtract).then_inc(wx_ready, 1)
            dve.wait_ge(wx_ready, 1)
            for k in range(KT):
                dve.tensor_copy(wrep_hi[:, k, :], wx_hi[:, k, SL:SL + 1].broadcast_to([P, P]))
                dve.tensor_copy(wrep_lo[:, k, :], wx_lo[:, k, SL:SL + 1].broadcast_to([P, P])).then_inc(wx_ready, 1)
            for k in range(KT):
                dve.wait_ge(w_high, k + 1)
                dve.scalar_tensor_tensor(out=w_lo[:, k, :, :], in0=w_sb[:, k, 1:3, :], scalar=W_SCALE,
                                         in1=w_hi[:, k, :, :], op0=ALU.mult, op1=ALU.subtract).then_inc(w_ready, 1)
            norm_group(0)
            for g in range(NG):
                tg = slice(g * GT, (g + 1) * GT)
                cols = slice(g * GT * P, (g + 1) * GT * P)
                if g + 1 < NG:
                    norm_group(g + 1)
                for k in range(KT):
                    dve.wait_ge(h0t_high, g * KT + k + 1)
                    dve.scalar_tensor_tensor(out=h0t_lo[:, k, cols], in0=t_bank(g, k), scalar=0.0,
                                             in1=h0t_hi[:, k, cols], op0=ALU.max, op1=ALU.subtract).then_inc(h0t_ready, 1)
                dve.wait_ge(narrow_product, g + 1)
                dve.tensor_copy(exs[:, tg, :], narrow_bank[:, :, 0:NX]).then_inc(narrow_copied, 1)
                dve.wait_ge(narrow_copied, g + 1)
                dve.tensor_scalar(sr_col[:, tg], exs[:, tg, SR], 1.0 / LO, None, ALU.mult)
                dve.tensor_scalar(factor_arg[:, tg, 0], exs[:, tg, SR], -SLOPE / LO, None, ALU.mult)
                dve.tensor_scalar(factor_arg[:, tg, 1], exs[:, tg, SL], SLOPE / LO, None, ALU.mult).then_inc(factor_args, 1)
                dve.tensor_scalar(mv_hi[:, tg, 1, D:D + 2], exs[:, tg, UA:UA + 2], 1.0 / LO, None, ALU.mult)\
                    .then_inc(narrow_high, 1)
                for m in range(2):
                    dve.tensor_scalar(gate_c[:, tg, m], exs[:, tg, CA + m], 1.0 / LO, c_sb[:, C_BAB + m:C_BAB + m + 1],
                                      ALU.mult, ALU.add)
                dve.wait_ge(narrow_high, g + 1)
                dve.scalar_tensor_tensor(out=mv_lo[:, tg, 1, D:D + 2], in0=mv_hi[:, tg, 1, D:D + 2], scalar=-LO,
                                         in1=exs[:, tg, UA:UA + 2], op0=ALU.mult, op1=ALU.add).then_inc(narrow_ready, 1)
                dve.wait_ge(factors_done, g + 1)
                dve.tensor_scalar(factor[:, tg, 1], factor[:, tg, 1], SUM_EPS * E_SCALE, None, ALU.mult).then_inc(eps_ready, 1)
                dve.wait_ge(adj_landed[0][g // 2], 16)
                for p in range(2 * g, 2 * g + 2):
                    mask_pair(dve, 0, p, p, p >= RING)
                for t in range(g * GT, (g + 1) * GT):
                    dve.wait_ge(wide_high, t + 1)
                    dve.scalar_tensor_tensor(out=mv_lo[:, t, :, 0:D], in0=mv_hi[:, t, :, 0:D], scalar=-LO,
                                             in1=wide_bank(t), op0=ALU.mult, op1=ALU.add).then_inc(wide_ready, 1)
                for p in range(2 * g, 2 * g + 2):
                    low_pair(dve, 0, p, p)
            dve.wait_ge(wide_ready, NT)
            dve.wait_ge(sl_ready, NG)
            dve.engine_nop().then_inc(banks_free, TPC)
            dve.wait_ge(eps_ready, NG)
            dve.wait_ge(xh_ready, NG)

            def step(slot, c, landed, tiles):
                for p in range(NP):
                    if p % (NP // 2) == 0:
                        dve.wait_ge(adj_landed[slot][p // (NP // 2)], landed)
                    mask_pair(dve, slot, p, c * NP + p, True)
                    if p:
                        low_pair(dve, slot, p - 1, c * NP + p - 1)
                    for at, q, n, t, stores in tiles:
                        if p == at:
                            dve_sum(dve, q, n, t)
                        if p == at + 1:
                            dve_logits(dve, q, n)
                        if p == at + 2:
                            dve_result(dve, q, n, t, stores)
                low_pair(dve, slot, NP - 1, c * NP + NP - 1)

            step(1, 1, 16, [(4, 0, 0, 0, None)])
            for r in range(NCH // 2 - 1):
                for s in range(2):
                    c = 2 * r + s + 2
                    n = (c - 2) * TPC + 1
                    step(s, c, 16 * (c // 2 + 1), [(0, 1, n, n, 16 * (c - 2)), (4, 0, n + 1, n + 1, 16 * (c - 1))])
            for n in range(NT - 3, NT):
                dve_sum(dve, n % 2, n, n)
                dve_logits(dve, n % 2, n)
                dve_result(dve, n % 2, n, n, 16 * (n // TPC))

        @block.tensor
        def _(pe):
            def turn_group(g):
                pe.wait_ge(normed, (g + 1) * GT)
                if g >= 2:
                    pe.wait_ge(h0t_ready, (g - 1) * KT)
                for k in range(KT):
                    for t in range(GT):
                        ins = pe.transpose(t_bank(g, k)[:, t * P:(t + 1) * P], xn[:, g % 2, t, k * P:(k + 1) * P], ident[:, :])
                ins.then_inc(turned, 1)

            pe.wait_ge(c_landed, 16)
            pe.wait_ge(w_landed, 16)
            for k in range(KT):
                for m in range(KT):
                    ins = pe.matmul(wl_bank[:, k, :], w_sb[:, m, 0, k * P:(k + 1) * P],
                                    c_sb[:, C_AVEC + 2 * m:C_AVEC + 2 * m + 2], start=(m == 0), stop=(m == KT - 1))
            ins.then_inc(wl_product, 1)
            pe.wait_ge(ident_ready, 2)
            turn_group(0)
            for g in range(NG):
                cols = slice(g * GT * P, (g + 1) * GT * P)
                if g + 1 < NG:
                    turn_group(g + 1)
                if g == 0:
                    pe.wait_ge(wx_ready, 1 + KT)
                pe.wait_ge(h0t_ready, (g + 1) * KT)
                if g >= 1:
                    pe.wait_ge(sl_ready, g)
                three = [(k, a, b) for k in range(KT) for a, b in ((0, 0), (0, 1), (1, 0))]
                for i, (k, a, b) in enumerate(three):
                    ins = pe.matmul(sl_bank, (wrep_hi, wrep_lo)[a][:, k, :], (h0t_hi, h0t_lo)[b][:, k, cols],
                                    start=(i == 0), stop=(i == len(three) - 1))
                ins.then_inc(sl_product, 1)
                if g >= 1:
                    pe.wait_ge(narrow_copied, g)
                for t in range(g * GT, (g + 1) * GT):
                    for i, (k, a, b) in enumerate(three):
                        ins = pe.matmul(narrow_bank[:, t % GT, 0:NX], (h0t_hi, h0t_lo)[a][:, k, t * P:(t + 1) * P],
                                        (wx_hi, wx_lo)[b][:, k, :], start=(i == 0), stop=(i == len(three) - 1))
                ins.then_inc(narrow_product, 1)
                if g == 0:
                    pe.wait_ge(w_ready, KT)
                for t in range(g * GT, (g + 1) * GT):
                    if t >= 2:
                        pe.wait_ge(wide_ready, t - 1)
                    for i, (k, a, b) in enumerate(three):
                        ins = pe.matmul(wide_bank(t), (h0t_hi, h0t_lo)[a][:, k, t * P:(t + 1) * P],
                                        (w_hi, w_lo)[b][:, k, :, :], start=(i == 0), stop=(i == len(three) - 1))
                    ins.then_inc(wide_product, 1)
            pe.wait_ge(wide_ready, NT)
            pe.wait_ge(narrow_ready, NG)
            pe.wait_ge(ones_ready, 2)

            def tile(slot, q, c):
                cols = slice(q * P, (q + 1) * P)
                pe.wait_ge(banks_free, c * TPC + q + 1)
                if q == 0:
                    pe.wait_ge(adj_landed[slot][0], (c // 2) * 16 + 16 if isinstance(c, int) else c * 8 + 16 - 8 * slot)
                    pe.wait_ge(adj_landed[slot][1], (c // 2) * 16 + 16 if isinstance(c, int) else c * 8 + 16 - 8 * slot)
                for j in range(NT):
                    pe.matmul(out_bank(q, 2)[:, 0:D + 2], adj16[:, slot, j, cols], mv_hi[:, j, 1, :],
                              start=(j == 0), stop=(j == NT - 1))
                    pe.matmul(out_bank(q, 3)[:, 0:D + 2], adj16[:, slot, j, cols], mv_lo[:, j, 1, :],
                              start=(j == 0), stop=(j == NT - 1))
                for j in range(NT):
                    if q == 0 and j % 2 == 0:
                        pe.wait_ge(e_ready, c * NP + j // 2 + 1)
                    pe.matmul(out_bank(q, 1)[:, 0:D + 1], e_lo[:, slot, j, cols], mv_hi[:, j, 0, 0:D + 1],
                              start=(j == 0), stop=False)
                    pe.matmul(out_bank(q, 1)[:, 0:D + 1], e_hi[:, slot, j, cols], mv_lo[:, j, 0, 0:D + 1],
                              start=False, stop=(j == NT - 1))
                    ins = pe.matmul(out_bank(q, 0)[:, 0:D + 1], e_hi[:, slot, j, cols], mv_hi[:, j, 0, 0:D + 1],
                                    start=(j == 0), stop=(j == NT - 1))
                ins.then_inc(tile_done, 1)

            with pe.Fori(0, NCH // 2) as r:
                for slot in range(2):
                    for q in range(TPC):
                        tile(slot, q, r * 2 + slot)


def kernel(x, adj, L0_gnn_W_sa, L0_gnn_a_sa, L0_gnn_W_gcnb, L0_gnn_b_gcnb, L0_gnn_Wa, L0_gnn_ba, L0_gnn_Wb, L0_gnn_bb):
    import numpy as np
    import concourse.bacc as bacc
    from concourse.bass_utils import run_bass_kernel_spmd

    x, adj, w_sa, a_sa, w_g, b_g, w_a, b_a, w_b, b_b = (np.asarray(a) for a in (
        x, adj, L0_gnn_W_sa, L0_gnn_a_sa, L0_gnn_W_gcnb, L0_gnn_b_gcnb, L0_gnn_Wa, L0_gnn_ba, L0_gnn_Wb, L0_gnn_bb))
    weights = np.stack([w_sa.T, w_sa, w_g]).reshape(3, KT, P, D).transpose(2, 1, 0, 3)
    a_vec = a_sa.reshape(2, KT, P).transpose(2, 1, 0).reshape(P, 2 * KT)
    halves = np.stack([w_a.reshape(2, D)[0], w_b.reshape(2, D)[0], w_a.reshape(2, D)[1], w_b.reshape(2, D)[1]])
    gates = halves.reshape(4, KT, P).transpose(2, 1, 0).reshape(P, 4 * KT)
    rows = [np.broadcast_to(v.reshape(1, -1), (P, v.size)) for v in (b_a, b_b, b_g)]
    consts = np.concatenate([a_vec, gates, *rows], axis=1)
    arrays = {"x": x, "adj_t": adj.T, "weights": weights, "consts": consts}
    arrays = {f"in_{k}": np.ascontiguousarray(v) for k, v in arrays.items()}

    nc = bacc.Bacc("TRN2", target_bir_lowering=False, num_devices=1)
    args = [nc.dram_tensor(k, v.shape, mybir.dt.from_np(v.dtype), kind="ExternalInput").ap() for k, v in arrays.items()]
    out = nc.dram_tensor("out", (N, D), F32, kind="ExternalOutput").ap()
    build(nc, *args, out)
    got = run_bass_kernel_spmd(nc, [arrays], core_ids=[0])
    return got.results[0]["out"]
```

```python
from contextlib import ExitStack
import math

import concourse.bass as bass
from concourse import mybir

F32 = mybir.dt.float32
F16 = mybir.dt.float16
I32 = mybir.dt.int32
ALU = mybir.AluOpType
ACT = mybir.ActivationFunctionType

P = 128
N = 2048
D = 256
NT = N // P
KT = D // P
GT = 4
NG = NT // GT
CW = 256
NCH = N // CW
TPC = CW // P
NP = NT // 2
HALF = NP // 2
RING = 4
LAG = 2
BANK = 512
SETS = 4

H0_SCALE = 2.0 ** 11
W_SCALE = 2.0 ** 5
PROD = H0_SCALE * W_SCALE
MV_SCALE = 2.0 ** 4
E_SCALE = 2.0 ** 15
FAR = 60000.0
LN_EPS = 1e-5
SUM_EPS = 1e-5
SLOPE = 0.01
MAGIC = float(0x5f3759df)

SL, SR, UA, UB, CA, CB = range(6)
NX = 6
C_AVEC, C_GATE, C_BAB, C_BIAS = 0, 4, 12, 14
C_WT = C_BIAS + D
C_END = C_WT + KT * D


def build(nc, x, adj_t, weights, consts, out):
    with ExitStack() as ctx:
        def sb(name, shape, dt):
            return ctx.enter_context(nc.sbuf_tensor(name, shape, dt))

        def sem(name):
            return ctx.enter_context(nc.semaphore(name))

        ps = ctx.enter_context(nc.psum_tensor("ps", [P, 8, BANK], F32))

        w_sb = sb("w_sb", [P, KT, 2, D], F32)
        c_sb = sb("c_sb", [P, C_END], F32)
        w_hi = sb("w_hi", [P, KT, 2, D], F16)
        w_lo = sb("w_lo", [P, KT, 2, D], F16)
        wx = sb("wx", [P, KT, NX], F32)
        wx_hi = sb("wx_hi", [P, KT, NX], F16)
        wx_lo = sb("wx_lo", [P, KT, NX], F16)
        wrep_hi = sb("wrep_hi", [P, KT, P], F16)
        wrep_lo = sb("wrep_lo", [P, KT, P], F16)
        ident = sb("ident", [P, P], F32)
        log_e = sb("log_e", [P, 1], F32)
        x_sb = sb("x_sb", [P, NT, D], F32)
        stats = sb("stats", [P, NT, 6], F32)
        mean_var = sb("mean_var", [P, NT, 2], F32)
        rstd = sb("rstd", [P, NT], F32)
        rs_v = sb("rs_v", [P, NT], F32)
        rs_a = sb("rs_a", [P, NT], F32)
        xn = sb("xn", [P, 2, GT, D], F32)
        h0t_hi = sb("h0t_hi", [P, KT, N], F16)
        h0t_lo = sb("h0t_lo", [P, KT, N], F16)
        mv_hi = sb("mv_hi", [P, NT, 2, D + 2], F16)
        mv_lo = sb("mv_lo", [P, NT, 2, D + 2], F16)
        exs = sb("exs", [P, NT, NX], F32)
        sr_col = sb("sr_col", [P, NT], F32)
        factor_arg = sb("factor_arg", [P, 2, NT], F32)
        factor = sb("factor", [P, 2, NT], F32)
        row_scale = sb("row_scale", [P, NT], F32)
        one_col = sb("one_col", [P, NT], F32)
        eps_col = sb("eps_col", [P, NT], F32)
        gate_c = sb("gate_c", [P, NT, 2], F32)
        sl_row = sb("sl_row", [P, N], F32)
        adj16 = sb("adj16", [P, 2, NT, CW], F16)
        far = sb("far", [P, 2, 2 * HALF, CW], F16)
        e_raw = sb("e_raw", [P, RING, 2, CW], F32)
        e_hi = sb("e_hi", [P, 2, NT, CW], F16)
        e_lo = sb("e_lo", [P, 2, NT, CW], F16)
        small = sb("small", [P, TPC, 10], F32)
        part_a = sb("part_a", [P, TPC, D], F32)
        part_b = sb("part_b", [P, TPC, D], F32)
        logit = sb("logit", [P, TPC, D], F32)
        tanh_v = sb("tanh_v", [P, TPC, D], F32)
        res = sb("res", [P, TPC, D], F32)

        w_landed = sem("w_landed")
        c_landed = sem("c_landed")
        x_landed = [sem(f"x_landed{g}") for g in range(NG)]
        adj_landed = [[sem(f"adj_landed{s}{h}") for h in range(2)] for s in range(2)]
        ident_ready = sem("ident_ready")
        consts_ready = sem("consts_ready")
        wl_product = sem("wl_product")
        wx_scaled = sem("wx_scaled")
        wx_high = sem("wx_high")
        wx_ready = sem("wx_ready")
        w_high = sem("w_high")
        w_ready = sem("w_ready")
        stats_done = sem("stats_done")
        moments_done = sem("moments_done")
        rstd_step = sem("rstd_step")
        normed = sem("normed")
        xh_ready = sem("xh_ready")
        turned = sem("turned")
        h0t_high = sem("h0t_high")
        h0t_ready = sem("h0t_ready")
        sl_product = sem("sl_product")
        sl_ready = sem("sl_ready")
        narrow_product = sem("narrow_product")
        narrow_copied = sem("narrow_copied")
        narrow_high = sem("narrow_high")
        narrow_ready = sem("narrow_ready")
        factor_args = sem("factor_args")
        factors_done = sem("factors_done")
        row_scaled = sem("row_scaled")
        wide_product = sem("wide_product")
        wide_high = sem("wide_high")
        wide_ready = sem("wide_ready")
        far_ready = sem("far_ready")
        z_done = sem("z_done")
        exp_done = sem("exp_done")
        e_high = sem("e_high")
        e_ready = sem("e_ready")
        banks_free = sem("banks_free")
        tile_done = sem("tile_done")
        gate_arg = sem("gate_arg")
        den_done = sem("den_done")
        rden_done = sem("rden_done")
        gate_tanh = sem("gate_tanh")
        gates_done = sem("gates_done")
        scale_done = sem("scale_done")
        a_scaled = sem("a_scaled")
        logits_done = sem("logits_done")
        tanh_done = sem("tanh_done")
        res_ready = sem("res_ready")
        res_free = [sem(f"res_free{q}") for q in range(TPC)]

        adj_v = adj_t.rearrange("(j p) i -> p j i", p=P)
        x_v = x.rearrange("(t p) d -> p t d", p=P)
        wt_sb = c_sb[:, C_WT:C_END].rearrange("p (k d) -> p k d", k=KT)

        def t_bank(g, k):
            return ps[:, 2 * (g % 2) + k, :]

        def wide_bank(t):
            return ps[:, 2 + t % 4, :].rearrange("p (m d) -> p m d", m=2)

        sl_bank = ps[:, 6, :]
        narrow_bank = ps[:, 7, 0:8 * NT].rearrange("p (t n) -> p t n", n=8)
        wl_bank = ps[:, 6, 0:2 * KT].rearrange("p (k n) -> p k n", k=KT)

        def out_bank(s, b):
            return ps[:, 2 * s + b, 0:D + 2]

        block = ctx.enter_context(nc.Block())

        @block.sync
        def _(sp):
            for g in range(NG):
                sp.dma_start(x_sb[:, g * GT:(g + 1) * GT, :], x_v[:, g * GT:(g + 1) * GT, :]).then_inc(x_landed[g], 16)
            sp.dma_start(w_sb[:, :, :, :], weights).then_inc(w_landed, 16)
            with sp.Fori(0, NCH) as c:
                for q in range(TPC):
                    sp.wait_ge(res_ready, c * TPC + q + 1)
                    sp.dma_start(out[bass.ds((c * TPC + q) * P, P), :], res[:, q, :]).then_inc(res_free[q], 16)
            for q in range(TPC):
                sp.wait_ge(res_free[q], 16 * NCH + 16)

        @block.gpsimd
        def _(pool):
            def load_adj(slot, c):
                for half in range(2):
                    js = slice(half * NT // 2, (half + 1) * NT // 2)
                    pool.dma_start(adj16[:, slot, js, :], adj_v[:, js, bass.ds(c * CW, CW)])\
                        .then_inc(adj_landed[slot][half], 16)

            pool.memset(ident[:, :], 0.0).then_inc(ident_ready, 1)
            pool.wait_ge(ident_ready, 1)
            pool.affine_select(out=ident[:, :], in_=ident[:, :], compare_op=ALU.not_equal, fill=1.0,
                               base=0, pattern=[[-1, P]], channel_multiplier=1).then_inc(ident_ready, 1)
            pool.wait_ge(x_landed[NG - 1], 16)
            load_adj(0, 0)
            load_adj(1, 1)
            for g in range(NG):
                pool.wait_ge(normed, (g + 1) * GT)
                xs = x_sb[:, g * GT:(g + 1) * GT, :]
                pool.tensor_scalar(xs, xs, 0.5, None, ALU.add).then_inc(xh_ready, 1)
            with pool.Fori(0, NCH // 2 - 1) as r:
                for slot in range(2):
                    pool.wait_ge(tile_done, r * 2 * TPC + (slot + 1) * TPC)
                    load_adj(slot, r * 2 + slot + 2)

        def dve_far(dve, c, c_slot, half, landed):
            dve.wait_ge(adj_landed[c_slot][half], landed)
            if not isinstance(c, int) or c >= 1:
                dve.wait_ge(z_done, c * NP - NP + (half + 1) * HALF)
            js = slice(half * 2 * HALF, (half + 1) * 2 * HALF)
            dve.tensor_scalar(far[:, half, :, :], adj16[:, c_slot, js, :], -FAR, FAR, ALU.mult, ALU.add)\
                .then_inc(far_ready, 1)

        def dve_z(dve, c, p):
            if not isinstance(c, int) or c * NP + p >= RING:
                dve.wait_ge(e_ready, c * NP + p - RING + 1)
            for u in range(2):
                j = 2 * p + u
                ins = dve.scalar_tensor_tensor(out=e_raw[:, p % RING, u, :], in0=sl_row[:, bass.ds(c * CW, CW)],
                                               scalar=sr_col[:, j:j + 1], in1=far[:, p // HALF, j % (2 * HALF), :],
                                               op0=ALU.add, op1=ALU.max)
            ins.then_inc(z_done, 1)

        def act_exp(act, p, n):
            act.wait_ge(z_done, n + 1)
            act.activation(e_raw[:, p % RING, :, :], e_raw[:, p % RING, :, :], ACT.Exp,
                           bias=log_e[:, 0:1], scale=SLOPE - 1.0).then_inc(exp_done, 1)

        def act_high(act, c_slot, p, n):
            act.wait_ge(exp_done, n + 1)
            act.activation(e_hi[:, c_slot, 2 * p:2 * p + 2, :], e_raw[:, p % RING, :, :], ACT.Copy).then_inc(e_high, 1)

        def dve_low(dve, c_slot, p, n):
            dve.wait_ge(e_high, n + 1)
            dve.tensor_tensor(e_lo[:, c_slot, 2 * p:2 * p + 2, :], e_raw[:, p % RING, :, :],
                              e_hi[:, c_slot, 2 * p:2 * p + 2, :], ALU.subtract).then_inc(e_ready, 1)

        def dve_den(dve, q, s, n, t):
            dve.wait_ge(tile_done, n + 1)
            dve.scalar_tensor_tensor(out=small[:, q:q + 1, 0:2], in0=ps[:, 2 * s + 1:2 * s + 2, D:D + 2], scalar=1.0 / MV_SCALE,
                                     in1=gate_c[:, bass.ds(t, 1), :], op0=ALU.mult, op1=ALU.add).then_inc(gate_arg, 1)
            dve.tensor_tensor(small[:, q, 4:5], out_bank(s, 0)[:, D:D + 1], eps_col[:, bass.ds(t, 1)], ALU.add).then_inc(den_done, 1)
            dve.scalar_tensor_tensor(out=part_b[:, q, :], in0=out_bank(s, 1)[:, 0:D], scalar=1.0 / MV_SCALE,
                                     in1=c_sb[:, C_BIAS:C_BIAS + D], op0=ALU.mult, op1=ALU.add)
            dve.wait_ge(den_done, n + 1)
            dve.reciprocal(small[:, q, 5:6], small[:, q, 4:5]).then_inc(rden_done, 1)

        def act_gates(act, q, n):
            act.wait_ge(gate_arg, n + 1)
            act.activation(small[:, q, 2:4], small[:, q, 0:2], ACT.Tanh, scale=0.5).then_inc(gate_tanh, 1)

        def dve_gates(dve, q, n):
            dve.wait_ge(gate_tanh, n + 1)
            dve.tensor_scalar(small[:, q, 6:8], small[:, q, 2:4], 0.5, 0.5, ALU.mult, ALU.add).then_inc(gates_done, 1)
            dve.wait_ge(rden_done, n + 1)
            dve.wait_ge(gates_done, n + 1)
            dve.tensor_tensor(small[:, q, 8:9], small[:, q, 6:7], small[:, q, 5:6], ALU.mult).then_inc(scale_done, 1)

        def act_scale(act, q, s, n):
            act.wait_ge(scale_done, n + 1)
            act.activation(part_a[:, q, :], out_bank(s, 0)[:, 0:D], ACT.Copy, scale=small[:, q, 8:9]).then_inc(a_scaled, 1)

        def dve_logit(dve, q, n):
            dve.wait_ge(a_scaled, n + 1)
            dve.scalar_tensor_tensor(out=logit[:, q, :], in0=part_b[:, q, :], scalar=small[:, q, 7:8],
                                     in1=part_a[:, q, :], op0=ALU.mult, op1=ALU.add).then_inc(logits_done, 1)
            dve.engine_nop().then_inc(banks_free, 1)

        def act_tanh(act, q, n):
            act.wait_ge(logits_done, n + 1)
            act.activation(tanh_v[:, q, :], logit[:, q, :], ACT.Tanh, scale=0.5).then_inc(tanh_done, 1)

        def dve_result(dve, q, n, t, stores):
            dve.wait_ge(tanh_done, n + 1)
            dve.wait_ge(res_free[q], stores + 16)
            dve.scalar_tensor_tensor(out=res[:, q:q + 1, :], in0=tanh_v[:, q:q + 1, :], scalar=0.5, in1=x_sb[:, bass.ds(t, 1), :],
                                     op0=ALU.mult, op1=ALU.add).then_inc(res_ready, 1)

        @block.scalar
        def _(act):
            act.dma_start(c_sb[:, :], consts).then_inc(c_landed, 16)
            act.wait_ge(w_landed, 16)
            for k in range(KT):
                act.activation(w_hi[:, k, :, :], w_sb[:, k, :, :], ACT.Copy, scale=W_SCALE).then_inc(w_high, 1)
            for g in range(NG):
                cols = slice(g * GT * P, (g + 1) * GT * P)
                act.wait_ge(turned, g + 1)
                for k in range(KT):
                    act.activation(h0t_hi[:, k, cols], t_bank(g, k), ACT.Relu).then_inc(h0t_high, 1)

            def copy_sl(g):
                act.wait_ge(sl_product, g + 1)
                act.activation(sl_row[:, g * GT * P:(g + 1) * GT * P], sl_bank, ACT.Copy, scale=1.0 / PROD).then_inc(sl_ready, 1)

            copy_sl(0)
            act.wait_ge(factor_args, 1)
            act.activation(factor[:, :, :], factor_arg[:, :, :], ACT.Exp).then_inc(factors_done, 1)
            act.wait_ge(consts_ready, 1)
            act.wait_ge(row_scaled, 1)
            for p in range(NP):
                act_exp(act, p, p)
                if p:
                    act_high(act, 0, p - 1, p - 1)
                for t in range(2 * p, 2 * p + 2):
                    act.wait_ge(wide_product, t + 1)
                    act.activation(mv_hi[:, t, 0, 0:D], wide_bank(t)[:, 0, :], ACT.Copy, scale=row_scale[:, t:t + 1])
                    act.activation(mv_hi[:, t, 1, 0:D], wide_bank(t)[:, 1, :], ACT.Copy, scale=MV_SCALE / PROD)\
                        .then_inc(wide_high, 1)
                if p % 2 and p // 2 + 1 < NG:
                    copy_sl(p // 2 + 1)

            def step(slot, c, m, s, whole):
                for p in range(NP):
                    n = c * NP + p
                    act_exp(act, p, n)
                    if p == 1 and whole:
                        act.wait_ge(tile_done, m + TPC)
                    act_high(act, slot if p else 1 - slot, (p - 1) % NP, n - 1)
                    if whole and p == 1:
                        act_tanh(act, 0, m)
                        act_gates(act, 1, m + 1)
                    if whole and p == 3:
                        act_scale(act, 1, (s + 1) % SETS, m + 1)
                    if whole and p == 5:
                        act_tanh(act, 1, m + 1)
                    if p == 5:
                        act_gates(act, 0, m + 2)
                    if p == 7:
                        act_scale(act, 0, (s + 2) % SETS, m + 2)

            step(1, 1, -TPC, -TPC, False)
            with act.Fori(0, NCH // 2 - 1) as r:
                for h in range(2):
                    step(h, r * 2 + h + 2, (r * 2 + h) * TPC, h * TPC, True)
            act_high(act, 1, NP - 1, NCH * NP - 1)
            act_tanh(act, 0, NT - 4)
            for n in range(NT - 3, NT):
                act_gates(act, n % 2, n)
                act_scale(act, n % 2, n % SETS, n)
                act_tanh(act, n % 2, n)

        @block.vector
        def _(dve):
            for q in range(TPC):
                dve.engine_nop().then_inc(res_free[q], 16)
            dve.memset(log_e[:, :], math.log(E_SCALE)).then_inc(consts_ready, 1)
            dve.wait_ge(c_landed, 16)
            dve.tensor_scalar(wx[:, :, UA:UA + 4], c_sb[:, C_GATE:C_GATE + 4 * KT].rearrange("p (k n) -> p k n", k=KT),
                              W_SCALE, None, ALU.mult).then_inc(wx_scaled, 1)
            dve.wait_ge(wl_product, 1)
            dve.tensor_scalar(wx[:, :, 0:2], wl_bank, W_SCALE, None, ALU.mult).then_inc(wx_scaled, 1)
            dve.wait_ge(wx_scaled, 2)
            dve.tensor_copy(wx_hi[:, :, :], wx[:, :, :]).then_inc(wx_high, 1)
            dve.wait_ge(wx_high, 1)
            dve.tensor_tensor(wx_lo[:, :, :], wx[:, :, :], wx_hi[:, :, :], ALU.subtract).then_inc(wx_ready, 1)
            dve.wait_ge(wx_ready, 1)
            for k in range(KT):
                dve.tensor_copy(wrep_hi[:, k, :], wx_hi[:, k, SL:SL + 1].broadcast_to([P, P]))
                dve.tensor_copy(wrep_lo[:, k, :], wx_lo[:, k, SL:SL + 1].broadcast_to([P, P])).then_inc(wx_ready, 1)
            for t in range(NT):
                if t % GT == 0:
                    dve.wait_ge(x_landed[t // GT], 16)
                dve.bn_stats(stats[:, t, :], x_sb[:, t, :]).then_inc(stats_done, 1)
            for t in range(NT):
                dve.wait_ge(stats_done, t + 1)
                dve.bn_aggr(mean_var[:, t, :], stats[:, t, :]).then_inc(moments_done, 1)
            v, y, a = rs_v[:, :], rstd[:, :], rs_a[:, :]
            dve.wait_ge(moments_done, NT)
            dve.tensor_scalar(v, mean_var[:, :, 1], LN_EPS, H0_SCALE ** -2, ALU.add, ALU.mult).then_inc(rstd_step, 1)
            dve.wait_ge(rstd_step, 1)
            dve.tensor_scalar(a.bitcast(I32), v.bitcast(I32), 1, None, ALU.logical_shift_right).then_inc(rstd_step, 1)
            dve.wait_ge(rstd_step, 2)
            dve.tensor_scalar(y.bitcast(I32), a.bitcast(I32), -1.0, MAGIC, ALU.mult, ALU.add).then_inc(rstd_step, 1)
            for i in range(3):
                dve.wait_ge(rstd_step, 3 * i + 3)
                dve.tensor_tensor(a, y, y, ALU.mult).then_inc(rstd_step, 1)
                dve.wait_ge(rstd_step, 3 * i + 4)
                dve.scalar_tensor_tensor(out=a, in0=a, scalar=-0.5, in1=v, op0=ALU.mult, op1=ALU.mult).then_inc(rstd_step, 1)
                dve.wait_ge(rstd_step, 3 * i + 5)
                dve.scalar_tensor_tensor(out=y, in0=a, scalar=1.5, in1=y, op0=ALU.add, op1=ALU.mult).then_inc(rstd_step, 1)
            dve.wait_ge(rstd_step, 12)

            def turned_low(g):
                cols = slice(g * GT * P, (g + 1) * GT * P)
                for k in range(KT):
                    dve.wait_ge(h0t_high, g * KT + k + 1)
                    dve.scalar_tensor_tensor(out=h0t_lo[:, k, cols], in0=t_bank(g, k), scalar=0.0,
                                             in1=h0t_hi[:, k, cols], op0=ALU.max, op1=ALU.subtract).then_inc(h0t_ready, 1)

            for g in range(NG):
                if g >= 2:
                    dve.wait_ge(turned, g - 1)
                for t in range(g * GT, (g + 1) * GT):
                    dve.tensor_scalar(xn[:, g % 2, t % GT, :], x_sb[:, t, :], mean_var[:, t, 0:1], rstd[:, t:t + 1],
                                      ALU.subtract, ALU.mult).then_inc(normed, 1)
                if g >= 1:
                    turned_low(g - 1)
            turned_low(NG - 1)
            for k in range(KT):
                dve.wait_ge(w_high, k + 1)
                dve.scalar_tensor_tensor(out=w_lo[:, k, :, :], in0=w_sb[:, k, :, :], scalar=W_SCALE,
                                         in1=w_hi[:, k, :, :], op0=ALU.mult, op1=ALU.subtract).then_inc(w_ready, 1)
            dve.wait_ge(narrow_product, 1)
            dve.tensor_scalar(exs[:, :, :], narrow_bank[:, :, 0:NX], 1.0 / PROD, None, ALU.mult).then_inc(narrow_copied, 1)
            dve.wait_ge(narrow_copied, 1)
            dve.tensor_scalar(factor_arg[:, 0, :], exs[:, :, SR], -SLOPE, None, ALU.mult)
            dve.tensor_scalar(factor_arg[:, 1, :], exs[:, :, SL], SLOPE, None, ALU.mult).then_inc(factor_args, 1)
            dve.tensor_copy(sr_col[:, :], exs[:, :, SR])
            dve.tensor_scalar(mv_hi[:, :, 1, D:D + 2], exs[:, :, UA:UA + 2], MV_SCALE, None, ALU.mult).then_inc(narrow_high, 1)
            for m in range(2):
                dve.tensor_scalar(gate_c[:, :, m], exs[:, :, CA + m], c_sb[:, C_BAB + m:C_BAB + m + 1], None, ALU.add)
            dve.wait_ge(factors_done, 1)
            dve.tensor_scalar(row_scale[:, :], factor[:, 0, :], MV_SCALE / PROD, None, ALU.mult)
            dve.tensor_scalar(eps_col[:, :], factor[:, 1, :], SUM_EPS * E_SCALE * MV_SCALE, None, ALU.mult)
            dve.tensor_scalar(one_col[:, :], factor[:, 0, :], MV_SCALE, None, ALU.mult).then_inc(row_scaled, 1)
            dve.wait_ge(narrow_high, 1)
            dve.scalar_tensor_tensor(out=mv_lo[:, :, 1, D:D + 2], in0=exs[:, :, UA:UA + 2], scalar=MV_SCALE,
                                     in1=mv_hi[:, :, 1, D:D + 2], op0=ALU.mult, op1=ALU.subtract)
            dve.wait_ge(row_scaled, 1)
            dve.tensor_copy(mv_hi[:, :, 0, D], one_col[:, :]).then_inc(narrow_high, 1)
            dve.wait_ge(narrow_high, 2)
            dve.tensor_tensor(mv_lo[:, :, 0, D], one_col[:, :], mv_hi[:, :, 0, D], ALU.subtract).then_inc(narrow_ready, 1)
            dve.wait_ge(narrow_ready, 1)
            dve.wait_ge(sl_ready, 1)
            for p in range(NP):
                if p % HALF == 0:
                    dve_far(dve, 0, 0, p // HALF, 16)
                    dve.wait_ge(far_ready, p // HALF + 1)
                dve_z(dve, 0, p)
                if p >= LAG:
                    dve_low(dve, 0, p - LAG, p - LAG)
                for t in range(2 * p, 2 * p + 2):
                    dve.wait_ge(wide_high, t + 1)
                    dve.scalar_tensor_tensor(out=mv_lo[:, t, 0, 0:D], in0=wide_bank(t)[:, 0, :], scalar=row_scale[:, t:t + 1],
                                             in1=mv_hi[:, t, 0, 0:D], op0=ALU.mult, op1=ALU.subtract)
                    dve.scalar_tensor_tensor(out=mv_lo[:, t, 1, 0:D], in0=wide_bank(t)[:, 1, :], scalar=MV_SCALE / PROD,
                                             in1=mv_hi[:, t, 1, 0:D], op0=ALU.mult, op1=ALU.subtract).then_inc(wide_ready, 1)
            dve.wait_ge(wide_ready, NT)
            dve.wait_ge(sl_ready, NG)
            dve.engine_nop().then_inc(banks_free, SETS)
            dve.wait_ge(xh_ready, NG)

            def step(slot, c, landed, m, s, stores, whole):
                for p in range(NP):
                    n = c * NP + p
                    if p % HALF == 0:
                        dve_far(dve, c, slot, p // HALF, landed)
                        dve.wait_ge(far_ready, c * 2 + p // HALF + 1)
                    dve_z(dve, c, p)
                    dve_low(dve, slot if p >= LAG else 1 - slot, (p - LAG) % NP, n - LAG)
                    if whole and p == 0:
                        dve_logit(dve, 0, m)
                        dve_den(dve, 1, (s + 1) % SETS, m + 1, m + 1)
                    if whole and p == 2:
                        dve_result(dve, 0, m, m, stores)
                        dve_gates(dve, 1, m + 1)
                    if whole and p == 4:
                        dve_logit(dve, 1, m + 1)
                    if p == 4:
                        dve_den(dve, 0, (s + 2) % SETS, m + 2, m + 2)
                    if whole and p == 6:
                        dve_result(dve, 1, m + 1, m + 1, stores)
                    if p == 6:
                        dve_gates(dve, 0, m + 2)

            step(1, 1, 16, -TPC, -TPC, 0, False)
            with dve.Fori(0, NCH // 2 - 1) as r:
                for h in range(2):
                    step(h, r * 2 + h + 2, (r + 2) * 16, (r * 2 + h) * TPC, h * TPC, (r * 2 + h) * 16, True)
            for i in range(LAG):
                dve_low(dve, 1, NP - LAG + i, NCH * NP - LAG + i)
            dve_logit(dve, 0, NT - 4)
            dve_result(dve, 0, NT - 4, NT - 4, 16 * (NCH - 2))
            for n in range(NT - 3, NT):
                dve_den(dve, n % 2, n % SETS, n, n)
                dve_gates(dve, n % 2, n)
                dve_logit(dve, n % 2, n)
                dve_result(dve, n % 2, n, n, 16 * (n // TPC))

        @block.tensor
        def _(pe):
            pe.wait_ge(c_landed, 16)
            for k in range(KT):
                for m in range(KT):
                    ins = pe.matmul(wl_bank[:, k, :], wt_sb[:, m, k * P:(k + 1) * P],
                                    c_sb[:, C_AVEC + 2 * m:C_AVEC + 2 * m + 2], start=(m == 0), stop=(m == KT - 1))
            ins.then_inc(wl_product, 1)
            three = [(k, a, b) for k in range(KT) for a, b in ((0, 0), (0, 1), (1, 0))]
            h0t = (h0t_hi, h0t_lo)

            def turn_group(g):
                if g >= 2:
                    pe.wait_ge(h0t_ready, (g - 1) * KT)
                for t in range(GT):
                    pe.wait_ge(normed, g * GT + t + 1)
                    for k in range(KT):
                        ins = pe.transpose(t_bank(g, k)[:, t * P:(t + 1) * P], xn[:, g % 2, t, k * P:(k + 1) * P], ident[:, :])
                ins.then_inc(turned, 1)

            def narrow(t):
                for i, (k, a, b) in enumerate(three):
                    ins = pe.matmul(narrow_bank[:, t, 0:NX], h0t[a][:, k, t * P:(t + 1) * P],
                                    (wx_hi, wx_lo)[b][:, k, :], start=(i == 0), stop=(i == len(three) - 1))
                return ins

            def sl_rows(g):
                if g:
                    pe.wait_ge(sl_ready, g)
                for i, (k, a, b) in enumerate(three):
                    ins = pe.matmul(sl_bank, (wrep_hi, wrep_lo)[a][:, k, :], h0t[b][:, k, g * GT * P:(g + 1) * GT * P],
                                    start=(i == 0), stop=(i == len(three) - 1))
                ins.then_inc(sl_product, 1)

            def wide(t):
                if t >= 4:
                    pe.wait_ge(wide_ready, t - 3)
                for i, (k, a, b) in enumerate(three):
                    ins = pe.matmul(wide_bank(t), h0t[a][:, k, t * P:(t + 1) * P],
                                    (w_hi, w_lo)[b][:, k, :, :], start=(i == 0), stop=(i == len(three) - 1))
                ins.then_inc(wide_product, 1)

            pe.wait_ge(ident_ready, 2)
            pe.wait_ge(wx_ready, 1 + KT)
            turn_group(0)
            for g in range(NG):
                if g + 1 < NG:
                    turn_group(g + 1)
                pe.wait_ge(h0t_ready, (g + 1) * KT)
                if g == 0:
                    sl_rows(0)
                for t in range(g * GT, (g + 1) * GT):
                    ins = narrow(t)
            ins.then_inc(narrow_product, 1)
            pe.wait_ge(w_ready, KT)
            for g in range(NG):
                for t in range(g * GT, (g + 1) * GT):
                    wide(t)
                if g + 1 < NG:
                    sl_rows(g + 1)
            pe.wait_ge(wide_ready, NT)
            pe.wait_ge(narrow_ready, 1)

            def tile(slot, q, c):
                cols = slice(q * P, (q + 1) * P)
                s = 2 * slot + q
                pe.wait_ge(banks_free, c * TPC + q + 1)
                if q == 0:
                    for half in range(2):
                        pe.wait_ge(adj_landed[slot][half], (c - slot) * 8 + 16)
                for j in range(NT):
                    pe.matmul(out_bank(s, 1), adj16[:, slot, j, cols], mv_hi[:, j, 1, :], start=(j == 0), stop=False)
                    pe.matmul(out_bank(s, 1), adj16[:, slot, j, cols], mv_lo[:, j, 1, :], start=False, stop=(j == NT - 1))
                for j in range(NT):
                    if q == 0 and j % 2 == 0:
                        pe.wait_ge(e_ready, c * NP + j // 2 + 1)
                    bank = out_bank(s, 0)[:, 0:D + 1]
                    pe.matmul(bank, e_hi[:, slot, j, cols], mv_lo[:, j, 0, 0:D + 1], start=(j == 0), stop=False)
                    pe.matmul(bank, e_hi[:, slot, j, cols], mv_hi[:, j, 0, 0:D + 1], start=False, stop=False)
                    ins = pe.matmul(bank, e_lo[:, slot, j, cols], mv_hi[:, j, 0, 0:D + 1], start=False, stop=(j == NT - 1))
                ins.then_inc(tile_done, 1)

            with pe.Fori(0, NCH // 2) as r:
                for slot in range(2):
                    for q in range(TPC):
                        tile(slot, q, r * 2 + slot)


def kernel(x, adj, L0_gnn_W_sa, L0_gnn_a_sa, L0_gnn_W_gcnb, L0_gnn_b_gcnb, L0_gnn_Wa, L0_gnn_ba, L0_gnn_Wb, L0_gnn_bb):
    import numpy as np
    import concourse.bacc as bacc
    from concourse.bass_utils import run_bass_kernel_spmd

    x, adj, w_sa, a_sa, w_g, b_g, w_a, b_a, w_b, b_b = (np.asarray(a) for a in (
        x, adj, L0_gnn_W_sa, L0_gnn_a_sa, L0_gnn_W_gcnb, L0_gnn_b_gcnb, L0_gnn_Wa, L0_gnn_ba, L0_gnn_Wb, L0_gnn_bb))
    weights = np.stack([w_sa, w_g]).reshape(2, KT, P, D).transpose(2, 1, 0, 3)
    wt = w_sa.T.reshape(KT, P, D).transpose(1, 0, 2).reshape(P, KT * D)
    a_vec = a_sa.reshape(2, KT, P).transpose(2, 1, 0).reshape(P, 2 * KT)
    halves = np.stack([w_a.reshape(2, D)[0], w_b.reshape(2, D)[0], w_a.reshape(2, D)[1], w_b.reshape(2, D)[1]])
    gates = halves.reshape(4, KT, P).transpose(2, 1, 0).reshape(P, 4 * KT)
    rows = [np.broadcast_to(v.reshape(1, -1), (P, v.size)) for v in (b_a, b_b, b_g)]
    consts = np.concatenate([a_vec, gates, *rows, wt], axis=1)
    arrays = {"x": x, "adj_t": adj.T, "weights": weights, "consts": consts}
    arrays = {f"in_{k}": np.ascontiguousarray(v) for k, v in arrays.items()}

    nc = bacc.Bacc("TRN2", target_bir_lowering=False, num_devices=1)
    args = [nc.dram_tensor(k, v.shape, mybir.dt.from_np(v.dtype), kind="ExternalInput").ap() for k, v in arrays.items()]
    out = nc.dram_tensor("out", (N, D), F32, kind="ExternalOutput").ap()
    build(nc, *args, out)
    got = run_bass_kernel_spmd(nc, [arrays], core_ids=[0])
    return got.results[0]["out"]
```

```python
from contextlib import ExitStack
import math

import concourse.bass as bass
from concourse import mybir

F32 = mybir.dt.float32
F16 = mybir.dt.float16
I32 = mybir.dt.int32
ALU = mybir.AluOpType
ACT = mybir.ActivationFunctionType

P = 128
N = 2048
D = 256
NT = N // P
KT = D // P
GT = 4
NG = NT // GT
CW = 256
NCH = N // CW
TPC = CW // P
NP = NT // 2
HALF = NP // 2
RING = 4
LAG = 2
BANK = 512
WB = 3

H0_SCALE = 2.0 ** 11
W_SCALE = 2.0 ** 5
PROD = H0_SCALE * W_SCALE
MV_SCALE = 2.0 ** 4
E_SCALE = 2.0 ** 15
FAR = 60000.0
LN_EPS = 1e-5
SUM_EPS = 1e-5
SLOPE = 0.01
MAGIC = float(0x5f3759df)

SL, SR, UA, UB, CA, CB = range(6)
NX = 6
C_AVEC, C_GATE, C_BAB, C_BIAS = 0, 4, 12, 14
C_WT = C_BIAS + D
C_END = C_WT + KT * D


def build(nc, x, adj_t, weights, consts, out):
    with ExitStack() as ctx:
        def sb(name, shape, dt):
            return ctx.enter_context(nc.sbuf_tensor(name, shape, dt))

        def sem(name):
            return ctx.enter_context(nc.semaphore(name))

        ps = ctx.enter_context(nc.psum_tensor("ps", [P, 8, BANK], F32))

        w_sb = sb("w_sb", [P, KT, 2, D], F32)
        c_sb = sb("c_sb", [P, C_END], F32)
        w_hi = sb("w_hi", [P, KT, 2, D], F16)
        w_lo = sb("w_lo", [P, KT, 2, D], F16)
        wx = sb("wx", [P, KT, NX], F32)
        wx_hi = sb("wx_hi", [P, KT, NX], F16)
        wx_lo = sb("wx_lo", [P, KT, NX], F16)
        ident = sb("ident", [P, P], F32)
        log_e = sb("log_e", [P, 1], F32)
        x_sb = sb("x_sb", [P, NT, D], F32)
        stats = sb("stats", [P, NT, 6], F32)
        mean_var = sb("mean_var", [P, NT, 2], F32)
        var_s = sb("var_s", [P, NT], F32)
        half_bits = sb("half_bits", [P, NT], F32)
        guess = sb("guess", [P, NT], F32)
        shift = sb("shift", [P, NT], F32)
        ratio = sb("ratio", [P, NT], F32)
        newton = sb("newton", [P, NT], F32)
        corr = sb("corr", [P, NT], F32)
        xn = sb("xn", [P, 2, GT, D], F32)
        h0t_hi = sb("h0t_hi", [P, KT, N], F16)
        h0t_lo = sb("h0t_lo", [P, KT, N], F16)
        mv_hi = sb("mv_hi", [P, NT, 2, D + 2], F16)
        mv_lo = sb("mv_lo", [P, NT, 2, D + 2], F16)
        exs = sb("exs", [P, NT, NX], F32)
        factor_r = sb("factor_r", [P, NT], F32)
        factor_l = sb("factor_l", [P, NT], F32)
        scale_a = sb("scale_a", [P, NT], F32)
        scale_b = sb("scale_b", [P, NT], F32)
        columns = sb("columns", [P, NT, 3], F32)
        eps_col = sb("eps_col", [P, NT], F32)
        gate_c = sb("gate_c", [P, NT, 2], F32)
        sl_row = sb("sl_row", [P, N], F32)
        adj16 = sb("adj16", [P, 2, NT, CW], F16)
        far = sb("far", [P, 2, 2 * HALF, CW], F16)
        e_raw = sb("e_raw", [P, RING, 2, CW], F32)
        e_hi = sb("e_hi", [P, NT, CW], F16)
        e_lo = sb("e_lo", [P, NT, CW], F16)
        gate_in = sb("gate_in", [P, 2, TPC, 2], F32)
        gate_t = sb("gate_t", [P, 2, TPC, 2], F32)
        gate_b = sb("gate_b", [P, 2, TPC], F32)
        den = sb("den", [P, 2, TPC], F32)
        rden = sb("rden", [P, 2, TPC], F32)
        weight_a = sb("weight_a", [P, 2, TPC], F32)
        part_b = sb("part_b", [P, TPC, D], F32)
        gated_b = sb("gated_b", [P, 2, TPC, D], F32)
        logit = sb("logit", [P, TPC, D], F32)
        res = sb("res", [P, 2, TPC, D], F32)

        w_landed = sem("w_landed")
        c_landed = sem("c_landed")
        x_landed = [sem(f"x_landed{g}") for g in range(NG)]
        adj_landed = [[sem(f"adj_landed{s}{h}") for h in range(2)] for s in range(2)]
        ident_ready = sem("ident_ready")
        consts_ready = sem("consts_ready")
        wl_product = sem("wl_product")
        wx_scaled = sem("wx_scaled")
        wx_high = sem("wx_high")
        wx_ready = sem("wx_ready")
        w_high = sem("w_high")
        w_ready = sem("w_ready")
        stats_done = sem("stats_done")
        moments_done = sem("moments_done")
        var_scaled = sem("var_scaled")
        bits_halved = sem("bits_halved")
        guess_ready = sem("guess_ready")
        shift_ready = sem("shift_ready")
        newton_step = sem("newton_step")
        corr_ready = sem("corr_ready")
        normed = sem("normed")
        xh_ready = sem("xh_ready")
        turned = sem("turned")
        h0t_high = sem("h0t_high")
        h0t_ready = sem("h0t_ready")
        narrow_product = sem("narrow_product")
        exs_ready = sem("exs_ready")
        factors_done = sem("factors_done")
        scales_ready = sem("scales_ready")
        columns_scaled = sem("columns_scaled")
        columns_high = sem("columns_high")
        narrow_ready = sem("narrow_ready")
        sl_turned = sem("sl_turned")
        sl_ready = sem("sl_ready")
        wide_product = sem("wide_product")
        wide_high = sem("wide_high")
        wide_ready = sem("wide_ready")
        far_ready = sem("far_ready")
        z_done = sem("z_done")
        exp_done = sem("exp_done")
        e_high = sem("e_high")
        e_ready = sem("e_ready")
        pair_used = sem("pair_used")
        b_done = sem("b_done")
        last_tile_done = sem("last_tile_done")
        gate_arg = sem("gate_arg")
        b_read = sem("b_read")
        gate_tanh = sem("gate_tanh")
        gate_b_done = sem("gate_b_done")
        b_gated = sem("b_gated")
        den_done = sem("den_done")
        rden_done = sem("rden_done")
        weight_done = sem("weight_done")
        a_read = sem("a_read")
        tanh_done = sem("tanh_done")
        res_ready = sem("res_ready")
        res_free = [sem(f"res_free{s}") for s in range(2)]

        adj_v = adj_t.rearrange("(j p) i -> p j i", p=P)
        x_v = x.rearrange("(t p) d -> p t d", p=P)
        out_v = out.rearrange("(t p) d -> p t d", p=P)
        wt_sb = c_sb[:, C_WT:C_END].rearrange("p (k d) -> p k d", k=KT)

        def t_bank(g, k):
            return ps[:, 2 * (g % 2) + k, :]

        def wide_bank(t):
            return ps[:, 4 + t % WB, :].rearrange("p (m d) -> p m d", m=2)

        narrow_bank = ps[:, 7, 0:8 * NT].rearrange("p (t n) -> p t n", n=8)
        wl_bank = ps[:, 7, 8 * NT:8 * NT + 2 * KT].rearrange("p (k n) -> p k n", k=KT)

        def a_bank(s, q):
            return ps[:, 4 * s + q, 0:D + 1]

        def b_bank(s, q):
            return ps[:, 4 * s + TPC + q, 0:D + 2]

        block = ctx.enter_context(nc.Block())

        @block.sync
        def _(sp):
            for g in range(NG):
                sp.dma_start(x_sb[:, g * GT:(g + 1) * GT, :], x_v[:, g * GT:(g + 1) * GT, :]).then_inc(x_landed[g], 16)
            with sp.Fori(0, NCH // 2 - 1) as r:
                for s in range(2):
                    c = r * 2 + s
                    sp.wait_ge(res_ready, c + 1)
                    sp.dma_start(out_v[:, bass.ds(c * TPC, TPC), :], res[:, s, :, :]).then_inc(res_free[s], 16)
            sp.wait_ge(res_ready, NCH - 1)
            sp.dma_start(out_v[:, NT - 2 * TPC:NT - TPC, :], res[:, 0, :, :]).then_inc(res_free[0], 16)
            for q in range(TPC):
                sp.wait_ge(res_ready, NCH + q)
                sp.dma_start(out_v[:, NT - TPC + q, :], res[:, 1, q, :]).then_inc(res_free[1], 16)
            for s in range(2):
                sp.wait_ge(res_free[s], 16 + 16 * (NCH // 2 + s * (TPC - 1)))

        @block.gpsimd
        def _(pool):
            def load_adj(s, c):
                for half in range(2):
                    js = slice(half * NT // 2, (half + 1) * NT // 2)
                    pool.dma_start(adj16[:, s, js, :], adj_v[:, js, bass.ds(c * CW, CW)])\
                        .then_inc(adj_landed[s][half], 16)

            def correct(g):
                ts = slice(g * GT, (g + 1) * GT)
                u, n, y = ratio[:, ts], newton[:, ts], corr[:, ts]
                step = g * 11
                pool.wait_ge(guess_ready, g + 1)
                pool.tensor_tensor(n, guess[:, ts], guess[:, ts], ALU.mult).then_inc(newton_step, 1)
                pool.wait_ge(newton_step, step + 1)
                pool.tensor_tensor(u, n, var_s[:, ts], ALU.mult).then_inc(newton_step, 1)
                pool.wait_ge(newton_step, step + 2)
                pool.tensor_scalar(y, u, -0.5, 1.5, ALU.mult, ALU.add).then_inc(newton_step, 1)
                for i in range(2):
                    step = g * 11 + 3 + 4 * i
                    pool.wait_ge(newton_step, step)
                    pool.tensor_tensor(n, y, y, ALU.mult).then_inc(newton_step, 1)
                    pool.wait_ge(newton_step, step + 1)
                    pool.tensor_tensor(n, n, u, ALU.mult).then_inc(newton_step, 1)
                    pool.wait_ge(newton_step, step + 2)
                    pool.tensor_scalar(n, n, -0.5, 1.5, ALU.mult, ALU.add).then_inc(newton_step, 1)
                    pool.wait_ge(newton_step, step + 3)
                    pool.tensor_tensor(y, y, n, ALU.mult).then_inc(newton_step, 1)
                pool.wait_ge(newton_step, g * 11 + 11)
                pool.tensor_scalar(scale_b[:, ts], y, MV_SCALE / PROD, None, ALU.mult).then_inc(corr_ready, 1)

            pool.memset(ident[:, :], 0.0).then_inc(ident_ready, 1)
            pool.wait_ge(ident_ready, 1)
            pool.affine_select(out=ident[:, :], in_=ident[:, :], compare_op=ALU.not_equal, fill=1.0,
                               base=0, pattern=[[-1, P]], channel_multiplier=1).then_inc(ident_ready, 1)
            correct(0)
            correct(1)
            pool.wait_ge(x_landed[NG - 1], 16)
            load_adj(0, 0)
            correct(2)
            load_adj(1, 1)
            correct(3)
            pool.wait_ge(factors_done, NG)
            pool.tensor_scalar(columns[:, :, 0], factor_r[:, :], MV_SCALE, None, ALU.mult)
            pool.tensor_scalar(columns[:, :, 1:3], exs[:, :, UA:UA + 2], MV_SCALE, None, ALU.mult).then_inc(columns_scaled, 1)
            pool.tensor_scalar(eps_col[:, :], factor_l[:, :], SUM_EPS * E_SCALE * MV_SCALE, None, ALU.mult)
            for m in range(2):
                pool.tensor_scalar(gate_c[:, :, m], exs[:, :, CA + m], c_sb[:, C_BAB + m:C_BAB + m + 1], None, ALU.add)
            pool.wait_ge(columns_scaled, 1)
            pool.tensor_copy(mv_hi[:, :, 0, D], columns[:, :, 0])
            pool.tensor_copy(mv_hi[:, :, 1, D:D + 2], columns[:, :, 1:3]).then_inc(columns_high, 1)
            pool.wait_ge(columns_high, 1)
            pool.tensor_tensor(mv_lo[:, :, 0, D], columns[:, :, 0], mv_hi[:, :, 0, D], ALU.subtract)
            pool.tensor_tensor(mv_lo[:, :, 1, D:D + 2], columns[:, :, 1:3], mv_hi[:, :, 1, D:D + 2], ALU.subtract)\
                .then_inc(narrow_ready, 1)
            for g in range(NG):
                pool.wait_ge(normed, (g + 1) * GT)
                xs = x_sb[:, g * GT:(g + 1) * GT, :]
                pool.tensor_scalar(xs, xs, 0.5, None, ALU.add).then_inc(xh_ready, 1)
            with pool.Fori(0, NCH // 2 - 1) as r:
                for s in range(2):
                    c = r * 2 + s
                    pool.wait_ge(b_done, (c + 1) * TPC)
                    pool.wait_ge(far_ready, (c + 1) * 2)
                    load_adj(s, c + 2)

        def dve_far(dve, c, s, half, landed):
            dve.wait_ge(adj_landed[s][half], landed)
            if not isinstance(c, int) or c >= 1:
                dve.wait_ge(z_done, c * NP - NP + (half + 1) * HALF)
            js = slice(half * 2 * HALF, (half + 1) * 2 * HALF)
            dve.tensor_scalar(far[:, half, :, :], adj16[:, s, js, :], -FAR, FAR, ALU.mult, ALU.add)\
                .then_inc(far_ready, 1)

        def dve_z(dve, c, p):
            if not isinstance(c, int) or c * NP + p >= RING:
                dve.wait_ge(e_ready, c * NP + p - RING + 1)
            for u in range(2):
                j = 2 * p + u
                ins = dve.scalar_tensor_tensor(out=e_raw[:, p % RING, u, :], in0=sl_row[:, bass.ds(c * CW, CW)],
                                               scalar=exs[:, j, SR:SR + 1], in1=far[:, p // HALF, j % (2 * HALF), :],
                                               op0=ALU.add, op1=ALU.max)
            ins.then_inc(z_done, 1)

        def act_exp(act, p, n):
            act.wait_ge(z_done, n + 1)
            act.activation(e_raw[:, p % RING, :, :], e_raw[:, p % RING, :, :], ACT.Exp,
                           bias=log_e[:, 0:1], scale=SLOPE - 1.0).then_inc(exp_done, 1)

        def act_high(act, p, n):
            if not isinstance(n, int) or n >= NP:
                act.wait_ge(pair_used, n - NP + 1)
            act.wait_ge(exp_done, n + 1)
            act.activation(e_hi[:, 2 * p:2 * p + 2, :], e_raw[:, p % RING, :, :], ACT.Copy).then_inc(e_high, 1)

        def dve_low(dve, p, n):
            dve.wait_ge(e_high, n + 1)
            dve.tensor_tensor(e_lo[:, 2 * p:2 * p + 2, :], e_raw[:, p % RING, :, :],
                              e_hi[:, 2 * p:2 * p + 2, :], ALU.subtract).then_inc(e_ready, 1)

        def dve_part_b(dve, c, s):
            dve.wait_ge(b_done, c * TPC + TPC)
            bank = ps[:, 4 * s + TPC:4 * s + 2 * TPC, :]
            dve.scalar_tensor_tensor(out=gate_in[:, s, :, :], in0=bank[:, :, D:D + 2], scalar=1.0 / MV_SCALE,
                                     in1=gate_c[:, bass.ds(c * TPC, TPC), :], op0=ALU.mult, op1=ALU.add).then_inc(gate_arg, 1)
            if not isinstance(c, int) or c >= 1:
                dve.wait_ge(b_gated, c * TPC)
            bias = c_sb[:, C_BIAS:C_BIAS + D].rearrange("p (o d) -> p o d", o=1).broadcast_to([P, TPC, D])
            dve.scalar_tensor_tensor(out=part_b[:, :, :], in0=bank[:, :, 0:D], scalar=1.0 / MV_SCALE,
                                     in1=bias, op0=ALU.mult, op1=ALU.add).then_inc(b_read, 1)

        def act_gates(act, c, s):
            act.wait_ge(gate_arg, c + 1)
            act.activation(gate_t[:, s, :, :], gate_in[:, s, :, :], ACT.Tanh, scale=0.5).then_inc(gate_tanh, 1)

        def dve_gate_b(dve, c, s):
            dve.wait_ge(gate_tanh, c + 1)
            dve.tensor_scalar(gate_b[:, s, :], gate_t[:, s, :, 1], 1.0, None, ALU.add).then_inc(gate_b_done, 1)

        def act_gated_b(act, c, s):
            act.wait_ge(b_read, c + 2)
            act.wait_ge(gate_b_done, c + 1)
            for q in range(TPC):
                act.activation(gated_b[:, s, q, :], part_b[:, q, :], ACT.Copy, scale=gate_b[:, s, q:q + 1]).then_inc(b_gated, 1)

        def dve_den(dve, c, s, q, nq, n):
            if nq == TPC:
                dve.wait_ge(pair_used, (c + 1) * NP)
            else:
                dve.wait_ge(last_tile_done, q + 1)
            dve.tensor_tensor(den[:, s, q:q + nq], ps[:, 4 * s + q:4 * s + q + nq, D], eps_col[:, bass.ds(c * TPC + q, nq)],
                              ALU.add).then_inc(den_done, 1)

        def dve_rden(dve, s, q, nq, n):
            dve.wait_ge(den_done, n + 1)
            dve.reciprocal(rden[:, s, q:q + nq], den[:, s, q:q + nq]).then_inc(rden_done, 1)

        def dve_weight_a(dve, c, s, q, nq, n):
            dve.wait_ge(rden_done, n + 1)
            dve.wait_ge(gate_tanh, c + 1)
            dve.scalar_tensor_tensor(out=weight_a[:, s, q:q + nq], in0=gate_t[:, s, q:q + nq, 0], scalar=1.0,
                                     in1=rden[:, s, q:q + nq], op0=ALU.add, op1=ALU.mult).then_inc(weight_done, 1)

        def dve_logit(dve, c, s, q, nq, n):
            dve.wait_ge(weight_done, n + 1)
            for qq in range(q, q + nq):
                dve.wait_ge(b_gated, c * TPC + qq + 1)
                ins = dve.scalar_tensor_tensor(out=logit[:, qq, :], in0=a_bank(s, qq)[:, 0:D], scalar=weight_a[:, s, qq:qq + 1],
                                               in1=gated_b[:, s, qq, :], op0=ALU.mult, op1=ALU.add)
            ins.then_inc(a_read, 1)

        def act_tanh(act, q, nq, n):
            act.wait_ge(a_read, n + 2)
            act.activation(logit[:, q:q + nq, :], logit[:, q:q + nq, :], ACT.Tanh, scale=0.25).then_inc(tanh_done, 1)

        def dve_result(dve, c, s, q, nq, n, stores):
            dve.wait_ge(tanh_done, n + 1)
            dve.wait_ge(res_free[s], 16 * stores + 16)
            dve.scalar_tensor_tensor(out=res[:, s, q:q + nq, :], in0=logit[:, q:q + nq, :], scalar=0.5,
                                     in1=x_sb[:, bass.ds(c * TPC + q, nq), :], op0=ALU.mult, op1=ALU.add).then_inc(res_ready, 1)

        @block.scalar
        def _(act):
            act.dma_start(c_sb[:, :], consts).then_inc(c_landed, 16)
            act.dma_start(w_sb[:, :, :, :], weights).then_inc(w_landed, 16)

            def norm(g):
                act.wait_ge(shift_ready, g + 1)
                if g >= 2:
                    act.wait_ge(turned, g - 1)
                for t in range(g * GT, (g + 1) * GT):
                    act.activation(xn[:, g % 2, t % GT, :], x_sb[:, t, :], ACT.Identity, bias=shift[:, t:t + 1],
                                   scale=guess[:, t:t + 1]).then_inc(normed, 1)

            def relu_high(g):
                act.wait_ge(turned, g + 1)
                for k in range(KT):
                    act.activation(h0t_hi[:, k, g * GT * P:(g + 1) * GT * P], t_bank(g, k), ACT.Relu).then_inc(h0t_high, 1)

            def factors(g):
                ts = slice(g * GT, (g + 1) * GT)
                act.wait_ge(exs_ready, g + 1)
                act.activation(factor_r[:, ts], exs[:, ts, SR], ACT.Exp, scale=-SLOPE)
                act.activation(factor_l[:, ts], exs[:, ts, SL], ACT.Exp, scale=SLOPE).then_inc(factors_done, 1)

            def wide_highs(g, half):
                act.wait_ge(scales_ready, g + 1)
                for t in range(g * GT + 2 * half, g * GT + 2 * half + 2):
                    act.wait_ge(wide_product, t + 1)
                    act.activation(mv_hi[:, t, 0, 0:D], wide_bank(t)[:, 0, :], ACT.Copy, scale=scale_a[:, t:t + 1])
                    act.activation(mv_hi[:, t, 1, 0:D], wide_bank(t)[:, 1, :], ACT.Copy, scale=scale_b[:, t:t + 1])\
                        .then_inc(wide_high, 1)

            def sl_rows(first, last, bank):
                cols = slice(first * CW, (last + 1) * CW)
                act.wait_ge(sl_turned, last + 1)
                act.activation(sl_row[:, cols], bank, ACT.Copy).then_inc(sl_ready, 1)

            def chunk0_w(p):
                act_exp(act, p, p)
                if p:
                    act_high(act, p - 1, p - 1)

            norm(0)
            act.wait_ge(w_landed, 16)
            for k in range(KT):
                act.activation(w_hi[:, k, :, :], w_sb[:, k, :, :], ACT.Copy, scale=W_SCALE).then_inc(w_high, 1)
            relu_high(0)
            norm(1)
            relu_high(1)
            factors(0)
            norm(2)
            act.wait_ge(consts_ready, 1)
            wide_highs(0, 0)
            factors(1)
            wide_highs(0, 1)
            relu_high(2)
            norm(3)
            wide_highs(1, 0)
            factors(2)
            sl_rows(0, 0, ps[:, 0, 0:CW])
            wide_highs(1, 1)
            chunk0_w(0)
            relu_high(3)
            wide_highs(2, 0)
            chunk0_w(1)
            factors(3)
            wide_highs(2, 1)
            chunk0_w(2)
            wide_highs(3, 0)
            chunk0_w(3)
            sl_rows(1, 1, ps[:, 0, CW:2 * CW])
            for b in range(1, NCH // 2):
                sl_rows(2 * b, 2 * b + 1, ps[:, b, :])
            wide_highs(3, 1)
            for p in range(4, NP):
                chunk0_w(p)

            def step(c, s, whole):
                for p in range(NP):
                    n = c * NP + p
                    act_exp(act, p, n)
                    act_high(act, (p - 1) % NP, n - 1)
                    if p == 1:
                        act_gates(act, c - 1, 1 - s)
                    if p == 4:
                        act_gated_b(act, c - 1, 1 - s)
                    if whole and p == 5:
                        act_tanh(act, 0, TPC, c - 2)

            step(1, 1, False)
            with act.Fori(0, NCH // 2 - 1) as r:
                for s in range(2):
                    step(r * 2 + s + 2, s, True)
            act_high(act, NP - 1, NCH * NP - 1)
            act_tanh(act, 0, TPC, NCH - 2)
            act_gates(act, NCH - 1, 1)
            act_gated_b(act, NCH - 1, 1)
            for q in range(TPC):
                act_tanh(act, q, 1, NCH - 1 + q)

        @block.vector
        def _(dve):
            for s in range(2):
                dve.engine_nop().then_inc(res_free[s], 16)
            dve.memset(log_e[:, :], math.log(E_SCALE)).then_inc(consts_ready, 1)

            def narrow_weights():
                dve.wait_ge(c_landed, 16)
                dve.tensor_scalar(wx[:, :, UA:UA + 4], c_sb[:, C_GATE:C_GATE + 4 * KT].rearrange("p (k n) -> p k n", k=KT),
                                  W_SCALE, None, ALU.mult).then_inc(wx_scaled, 1)
                dve.wait_ge(wl_product, 1)
                dve.tensor_scalar(wx[:, :, 0:2], wl_bank, W_SCALE, None, ALU.mult).then_inc(wx_scaled, 1)
                dve.wait_ge(wx_scaled, 2)
                dve.tensor_copy(wx_hi[:, :, :], wx[:, :, :]).then_inc(wx_high, 1)
                dve.wait_ge(wx_high, 1)
                dve.tensor_tensor(wx_lo[:, :, :], wx[:, :, :], wx_hi[:, :, :], ALU.subtract).then_inc(wx_ready, 1)

            def moments(g):
                dve.wait_ge(x_landed[g], 16)
                for t in range(g * GT, (g + 1) * GT):
                    dve.bn_stats(stats[:, t, :], x_sb[:, t, :]).then_inc(stats_done, 1)
                for t in range(g * GT, (g + 1) * GT):
                    dve.wait_ge(stats_done, t + 1)
                    dve.bn_aggr(mean_var[:, t, :], stats[:, t, :]).then_inc(moments_done, 1)

            def guesses(g):
                ts = slice(g * GT, (g + 1) * GT)
                dve.wait_ge(moments_done, (g + 1) * GT)
                dve.tensor_scalar(var_s[:, ts], mean_var[:, ts, 1], LN_EPS, H0_SCALE ** -2, ALU.add, ALU.mult).then_inc(var_scaled, 1)
                dve.wait_ge(var_scaled, g + 1)
                dve.tensor_scalar(half_bits[:, ts].bitcast(I32), var_s[:, ts].bitcast(I32), 1, None,
                                  ALU.logical_shift_right).then_inc(bits_halved, 1)
                dve.wait_ge(bits_halved, g + 1)
                dve.tensor_scalar(guess[:, ts].bitcast(I32), half_bits[:, ts].bitcast(I32), -1.0, MAGIC,
                                  ALU.mult, ALU.add).then_inc(guess_ready, 1)
                dve.wait_ge(guess_ready, g + 1)
                dve.scalar_tensor_tensor(out=shift[:, ts], in0=mean_var[:, ts, 0], scalar=-1.0, in1=guess[:, ts],
                                         op0=ALU.mult, op1=ALU.mult).then_inc(shift_ready, 1)

            def relu_low(g):
                for k in range(KT):
                    cols = slice(g * GT * P, (g + 1) * GT * P)
                    dve.wait_ge(h0t_high, g * KT + k + 1)
                    dve.scalar_tensor_tensor(out=h0t_lo[:, k, cols], in0=t_bank(g, k), scalar=0.0,
                                             in1=h0t_hi[:, k, cols], op0=ALU.max, op1=ALU.subtract).then_inc(h0t_ready, 1)

            def narrow_results(g):
                ts = slice(g * GT, (g + 1) * GT)
                dve.wait_ge(narrow_product, g + 1)
                dve.wait_ge(corr_ready, g + 1)
                cb = corr[:, ts].rearrange("p (t o) -> p t o", o=1).broadcast_to([P, GT, NX])
                dve.scalar_tensor_tensor(out=exs[:, ts, :], in0=narrow_bank[:, ts, 0:NX], scalar=1.0 / PROD, in1=cb,
                                         op0=ALU.mult, op1=ALU.mult).then_inc(exs_ready, 1)

            def row_scales(g):
                ts = slice(g * GT, (g + 1) * GT)
                dve.wait_ge(factors_done, g + 1)
                dve.tensor_tensor(scale_a[:, ts], factor_r[:, ts], scale_b[:, ts], ALU.mult).then_inc(scales_ready, 1)

            def wide_lows(g, half):
                dve.wait_ge(scales_ready, g + 1)
                for t in range(g * GT + 2 * half, g * GT + 2 * half + 2):
                    dve.wait_ge(wide_high, t + 1)
                    dve.scalar_tensor_tensor(out=mv_lo[:, t, 0, 0:D], in0=wide_bank(t)[:, 0, :], scalar=scale_a[:, t:t + 1],
                                             in1=mv_hi[:, t, 0, 0:D], op0=ALU.mult, op1=ALU.subtract)
                    dve.scalar_tensor_tensor(out=mv_lo[:, t, 1, 0:D], in0=wide_bank(t)[:, 1, :], scalar=scale_b[:, t:t + 1],
                                             in1=mv_hi[:, t, 1, 0:D], op0=ALU.mult, op1=ALU.subtract).then_inc(wide_ready, 1)

            def chunk0_w(p):
                if p % HALF == 0:
                    dve_far(dve, 0, 0, p // HALF, 16)
                    dve.wait_ge(far_ready, p // HALF + 1)
                if p == 0:
                    dve.wait_ge(sl_ready, 1)
                dve.wait_ge(exs_ready, 2 * p // GT + 1)
                dve_z(dve, 0, p)
                if p >= LAG:
                    dve_low(dve, p - LAG, p - LAG)

            moments(0)
            guesses(0)
            narrow_weights()
            moments(1)
            guesses(1)
            for k in range(KT):
                dve.wait_ge(w_high, k + 1)
                dve.scalar_tensor_tensor(out=w_lo[:, k, :, :], in0=w_sb[:, k, :, :], scalar=W_SCALE,
                                         in1=w_hi[:, k, :, :], op0=ALU.mult, op1=ALU.subtract).then_inc(w_ready, 1)
            relu_low(0)
            moments(2)
            narrow_results(0)
            guesses(2)
            row_scales(0)
            relu_low(1)
            moments(3)
            guesses(3)
            wide_lows(0, 0)
            narrow_results(1)
            wide_lows(0, 1)
            row_scales(1)
            relu_low(2)
            wide_lows(1, 0)
            narrow_results(2)
            chunk0_w(0)
            wide_lows(1, 1)
            row_scales(2)
            relu_low(3)
            chunk0_w(1)
            wide_lows(2, 0)
            narrow_results(3)
            chunk0_w(2)
            wide_lows(2, 1)
            row_scales(3)
            chunk0_w(3)
            wide_lows(3, 0)
            chunk0_w(4)
            wide_lows(3, 1)
            for p in range(5, NP):
                chunk0_w(p)

            def step(c, s, landed, whole, stores):
                for p in range(NP):
                    if p % HALF == 0:
                        dve_far(dve, c, s, p // HALF, landed)
                        dve.wait_ge(far_ready, c * 2 + p // HALF + 1)
                    dve_z(dve, c, p)
                    dve_low(dve, (p - LAG) % NP, c * NP + p - LAG)
                    if p == 0:
                        dve_part_b(dve, c - 1, 1 - s)
                    if p == 2:
                        dve_gate_b(dve, c - 1, 1 - s)
                    if whole and p == 0:
                        dve_den(dve, c - 2, s, 0, TPC, c - 2)
                    if whole and p == 1:
                        dve_rden(dve, s, 0, TPC, c - 2)
                    if whole and p == 2:
                        dve_weight_a(dve, c - 2, s, 0, TPC, c - 2)
                    if whole and p == 3:
                        dve_logit(dve, c - 2, s, 0, TPC, c - 2)
                    if whole and p == 6:
                        dve_result(dve, c - 2, s, 0, TPC, c - 2, stores)

            dve.wait_ge(wide_ready, NT)
            dve.engine_nop().then_inc(a_read, 1)
            dve.engine_nop().then_inc(b_read, 1)
            dve.wait_ge(sl_ready, 1 + NCH // 2)
            dve.wait_ge(narrow_ready, 1)
            step(1, 1, 16, False, 0)
            dve.wait_ge(xh_ready, NG)
            with dve.Fori(0, NCH // 2 - 1) as r:
                for s in range(2):
                    step(r * 2 + s + 2, s, r * 16 + 32, True, r)
            for p in range(NP - LAG, NP):
                dve_low(dve, p, NCH * NP - NP + p)
            last = NCH - 1
            dve_den(dve, last - 1, 0, 0, TPC, last - 1)
            dve_rden(dve, 0, 0, TPC, last - 1)
            dve_weight_a(dve, last - 1, 0, 0, TPC, last - 1)
            dve_logit(dve, last - 1, 0, 0, TPC, last - 1)
            dve_part_b(dve, last, 1)
            dve_result(dve, last - 1, 0, 0, TPC, last - 1, NCH // 2 - 1)
            dve_gate_b(dve, last, 1)
            for q in range(TPC):
                dve_den(dve, last, 1, q, 1, last + q)
                dve_rden(dve, 1, q, 1, last + q)
                dve_weight_a(dve, last, 1, q, 1, last + q)
                dve_logit(dve, last, 1, q, 1, last + q)
                dve_result(dve, last, 1, q, 1, last + q, NCH // 2 - 1)

        @block.tensor
        def _(pe):
            pe.wait_ge(c_landed, 16)
            for k in range(KT):
                for m in range(KT):
                    ins = pe.matmul(wl_bank[:, k, :], wt_sb[:, m, k * P:(k + 1) * P],
                                    c_sb[:, C_AVEC + 2 * m:C_AVEC + 2 * m + 2], start=(m == 0), stop=(m == KT - 1))
            ins.then_inc(wl_product, 1)
            three = [(k, a, b) for k in range(KT) for a, b in ((0, 0), (0, 1), (1, 0))]
            h0t = (h0t_hi, h0t_lo)

            def turn(g):
                if g >= 2:
                    pe.wait_ge(h0t_ready, (g - 1) * KT)
                for t in range(GT):
                    pe.wait_ge(normed, g * GT + t + 1)
                    for k in range(KT):
                        ins = pe.transpose(t_bank(g, k)[:, t * P:(t + 1) * P], xn[:, g % 2, t, k * P:(k + 1) * P], ident[:, :])
                ins.then_inc(turned, 1)

            def narrow(g):
                pe.wait_ge(h0t_ready, (g + 1) * KT)
                for t in range(g * GT, (g + 1) * GT):
                    for i, (k, a, b) in enumerate(three):
                        ins = pe.matmul(narrow_bank[:, t, 0:NX], h0t[a][:, k, t * P:(t + 1) * P],
                                        (wx_hi, wx_lo)[b][:, k, :], start=(i == 0), stop=(i == len(three) - 1))
                ins.then_inc(narrow_product, 1)

            def sl_rows(c):
                bank = ps[:, c // 2, (c % 2) * CW:(c % 2 + 1) * CW]
                pe.wait_ge(exs_ready, c * TPC // GT + 1)
                pe.wait_ge(h0t_ready, (NG if c else 3) * KT)
                if c == 1:
                    pe.wait_ge(sl_ready, 1)
                for q in range(TPC):
                    ins = pe.transpose(bank[:, q * P:(q + 1) * P], exs[:, c * TPC + q, SL:SL + 1].broadcast_to([P, P]),
                                       ident[:, :])
                ins.then_inc(sl_turned, 1)

            def wide(g, half):
                for t in range(g * GT + 2 * half, g * GT + 2 * half + 2):
                    if t >= WB:
                        pe.wait_ge(wide_ready, t - WB + 1)
                    for i, (k, a, b) in enumerate(three):
                        ins = pe.matmul(wide_bank(t), h0t[a][:, k, t * P:(t + 1) * P],
                                        (w_hi, w_lo)[b][:, k, :, :], start=(i == 0), stop=(i == len(three) - 1))
                    ins.then_inc(wide_product, 1)

            pe.wait_ge(ident_ready, 2)
            turn(0)
            turn(1)
            pe.wait_ge(wx_ready, 1)
            narrow(0)
            pe.wait_ge(w_ready, KT)
            wide(0, 0)
            narrow(1)
            wide(0, 1)
            turn(2)
            wide(1, 0)
            narrow(2)
            sl_rows(0)
            wide(1, 1)
            turn(3)
            wide(2, 0)
            narrow(3)
            wide(2, 1)
            wide(3, 0)
            for c in range(1, NCH):
                sl_rows(c)
            wide(3, 1)
            pe.wait_ge(sl_ready, 1 + NCH // 2)
            pe.wait_ge(narrow_ready, 1)

            def adj_products(c, s, q):
                for j in range(NT):
                    if isinstance(c, int) and c == 0 and q == 0:
                        pe.wait_ge(wide_ready, j + 1)
                    cols = slice(q * P, (q + 1) * P)
                    pe.matmul(b_bank(s, q), adj16[:, s, j, cols], mv_hi[:, j, 1, :], start=(j == 0), stop=False)
                    ins = pe.matmul(b_bank(s, q), adj16[:, s, j, cols], mv_lo[:, j, 1, :], start=False, stop=(j == NT - 1))
                ins.then_inc(b_done, 1)

            def w_products(s, q, j):
                cols = slice(q * P, (q + 1) * P)
                pe.matmul(a_bank(s, q), e_hi[:, j, cols], mv_lo[:, j, 0, 0:D + 1], start=(j == 0), stop=False)
                pe.matmul(a_bank(s, q), e_hi[:, j, cols], mv_hi[:, j, 0, 0:D + 1], start=False, stop=False)
                return pe.matmul(a_bank(s, q), e_lo[:, j, cols], mv_hi[:, j, 0, 0:D + 1], start=False, stop=(j == NT - 1))

            def chunk(c, s, landed):
                if not isinstance(c, int) or c >= 1:
                    pe.wait_ge(b_read, c)
                for half in range(2):
                    pe.wait_ge(adj_landed[s][half], landed)
                for q in range(TPC):
                    adj_products(c, s, q)
                if not isinstance(c, int) or c >= 1:
                    pe.wait_ge(a_read, c)
                if isinstance(c, int) and c == NCH - 1:
                    for q in range(TPC):
                        for j in range(NT):
                            if q == 0 and j % 2 == 0:
                                pe.wait_ge(e_ready, c * NP + j // 2 + 1)
                            ins = w_products(s, q, j)
                        ins.then_inc(last_tile_done, 1)
                    return
                for j in range(NT):
                    if j % 2 == 0:
                        pe.wait_ge(e_ready, c * NP + j // 2 + 1)
                    for q in range(TPC):
                        ins = w_products(s, q, j)
                    if j % 2 == 1:
                        ins.then_inc(pair_used, 1)

            chunk(0, 0, 16)
            with pe.Fori(0, NCH // 2 - 1) as r:
                chunk(r * 2 + 1, 1, r * 16 + 16)
                chunk(r * 2 + 2, 0, r * 16 + 32)
            chunk(NCH - 1, 1, 16 * NCH // 2)


def kernel(x, adj, L0_gnn_W_sa, L0_gnn_a_sa, L0_gnn_W_gcnb, L0_gnn_b_gcnb, L0_gnn_Wa, L0_gnn_ba, L0_gnn_Wb, L0_gnn_bb):
    import numpy as np
    import concourse.bacc as bacc
    from concourse.bass_utils import run_bass_kernel_spmd

    x, adj, w_sa, a_sa, w_g, b_g, w_a, b_a, w_b, b_b = (np.asarray(a) for a in (
        x, adj, L0_gnn_W_sa, L0_gnn_a_sa, L0_gnn_W_gcnb, L0_gnn_b_gcnb, L0_gnn_Wa, L0_gnn_ba, L0_gnn_Wb, L0_gnn_bb))
    weights = np.stack([w_sa, w_g]).reshape(2, KT, P, D).transpose(2, 1, 0, 3)
    wt = w_sa.T.reshape(KT, P, D).transpose(1, 0, 2).reshape(P, KT * D)
    a_vec = a_sa.reshape(2, KT, P).transpose(2, 1, 0).reshape(P, 2 * KT)
    halves = np.stack([w_a.reshape(2, D)[0], w_b.reshape(2, D)[0], w_a.reshape(2, D)[1], w_b.reshape(2, D)[1]])
    gates = halves.reshape(4, KT, P).transpose(2, 1, 0).reshape(P, 4 * KT)
    rows = [np.broadcast_to(v.reshape(1, -1), (P, v.size)) for v in (b_a, b_b, b_g)]
    consts = np.concatenate([a_vec, gates, *rows, wt], axis=1)
    arrays = {"x": x, "adj_t": adj.T, "weights": weights, "consts": consts}
    arrays = {f"in_{k}": np.ascontiguousarray(v) for k, v in arrays.items()}

    nc = bacc.Bacc("TRN2", target_bir_lowering=False, num_devices=1)
    args = [nc.dram_tensor(k, v.shape, mybir.dt.from_np(v.dtype), kind="ExternalInput").ap() for k, v in arrays.items()]
    out = nc.dram_tensor("out", (N, D), F32, kind="ExternalOutput").ap()
    build(nc, *args, out)
    got = run_bass_kernel_spmd(nc, [arrays], core_ids=[0])
    return got.results[0]["out"]
```
